# Optimizing a Trainium2 kernel written in Bass

```python
import numpy as np
import jax
import jax.numpy as jnp

def _softmax(x, axis=-1):
    return jax.nn.softmax(x, axis=axis)

def _gelu(x):
    return jax.nn.gelu(x, approximate=True)

def _silu(x):
    return jax.nn.silu(x)

def _sigmoid(x):
    return jax.nn.sigmoid(x)

def _layernorm(x, axis=-1, eps=1e-05):
    m = jnp.mean(x, axis=axis, keepdims=True)
    v = jnp.var(x, axis=axis, keepdims=True)
    return (x - m) / jnp.sqrt(v + eps)

def _scatter_add(tgt, idx, src, axis=0):
    return tgt.at[idx].add(src)

def _segment_sum(src, seg, n):
    return jax.ops.segment_sum(src, seg, n)
kernel_name = 'mk_xattn_ffn_d1_seqx_r4_e81f76'

def setup_inputs(seed: int=0):
    np.random.seed(seed)
    _w = jnp.asarray

    def _rec_inputs():
        import jax
        import jax.numpy as jnp
        _rk = jax.random.key(seed)
        x = -0.0003929 + 0.9999 * jax.random.normal(jax.random.fold_in(_rk, 1), (16, 100, 512), jnp.float32)
        _lenS = 100 - jax.random.randint(jax.random.fold_in(_rk, 7), (16,), 0, max(1, 100 // 4) + 1, jnp.int32)
        _lenS2 = 361 - jax.random.randint(jax.random.fold_in(_rk, 8), (16,), 0, max(1, 361 // 4) + 1, jnp.int32)
        _ctx_1024P = jax.random.normal(jax.random.fold_in(_rk, 11), (16, 16, 256), jnp.float32)
        _ctx_1024c = jax.random.dirichlet(jax.random.fold_in(_rk, 511), 0.3 * jnp.ones((16,), jnp.float32), (16, 361))
        _ctx_1024t = jnp.einsum('bsk,bkd->bsd', _ctx_1024c, _ctx_1024P)
        _ctx_1024t = _ctx_1024t * jax.lax.rsqrt(jnp.mean(jnp.square(_ctx_1024t)) + 1e-12) * 0.953939
        ctx_1024 = 0.000227908 + 0.99994 * (_ctx_1024t + 0.3 * jax.random.normal(jax.random.fold_in(_rk, 611), (16, 361, 256), jnp.float32))
        return (x, ctx_1024)
    x, ctx_1024 = _rec_inputs()

    def _L0_xattn_setup():
        import jax, jax.numpy as jnp
        import numpy as np
        EPS = 1e-05

        def rmsnorm(x, g, eps=EPS):
            var = jnp.mean(jnp.square(x), axis=-1, keepdims=True)
            return x * jax.lax.rsqrt(var + eps) * g
        key = jax.random.key(seed)
        ks = jax.random.split(key, 8)
        B, Sq, Skv = (2, 1024, 128)
        dim, cdim, H, D = (512, 256, 16, 128)
        inner = H * D
        s = lambda f: 1.0 / np.sqrt(f)
        return {'hidden_states': jax.random.normal(ks[0], (B, Sq, dim), jnp.float32), 'encoder_hidden_states': jax.random.normal(ks[1], (B, Skv, cdim), jnp.float32), 'Wq': jax.random.normal(ks[2], (dim, inner), jnp.float32) * s(dim), 'Wk': jax.random.normal(ks[3], (cdim, inner), jnp.float32) * s(cdim), 'Wv': jax.random.normal(ks[4], (cdim, inner), jnp.float32) * s(cdim), 'Wo': jax.random.normal(ks[5], (inner, dim), jnp.float32) * s(inner), 'gq': jnp.ones((D,), jnp.float32), 'gk': jnp.ones((D,), jnp.float32)}
    _L0_xattn_all = _L0_xattn_setup()
    _L0_xattn_in = {k: v for k, v in _L0_xattn_all.items() if k in ('Wq', 'Wk', 'Wv', 'Wo', 'gq', 'gk')}
    del _L0_xattn_all

    def _L0_ffn_setup():
        import jax, jax.numpy as jnp
        import numpy as np
        BLOCK_SIZE = 32
        HIDDEN_SIZE = 512
        MLP_DIM = 4096
        NVFP4_LUT = jnp.array([0.0, 0.5, 1.0, 1.5, 2.0, 3.0, 4.0, 6.0, 0.0, -0.5, -1.0, -1.5, -2.0, -3.0, -4.0, -6.0], dtype=jnp.float32)

        def dequant_nvfp4(W_packed, scales, block=BLOCK_SIZE):
            N = W_packed.shape[0]
            low = W_packed & 15
            high = W_packed >> 4 & 15
            idx = jnp.stack([low, high], axis=-1).reshape(N, -1)
            vals = NVFP4_LUT[idx]
            K = vals.shape[1]
            vals = vals.reshape(N, K // block, block) * scales[:, :, None]
            return vals.reshape(N, K)
        key = jax.random.key(seed)
        ks = jax.random.split(key, 7)
        x = jax.random.normal(ks[0], (4, 32, HIDDEN_SIZE), dtype=jnp.float32)
        gate_W_packed = jax.random.randint(ks[1], (MLP_DIM, HIDDEN_SIZE // 2), 0, 64, dtype=jnp.int32)
        gate_scales = jax.random.uniform(ks[2], (MLP_DIM, HIDDEN_SIZE // BLOCK_SIZE), dtype=jnp.float32) * 0.1 + 0.001
        up_W_packed = jax.random.randint(ks[3], (MLP_DIM, HIDDEN_SIZE // 2), 0, 64, dtype=jnp.int32)
        up_scales = jax.random.uniform(ks[4], (MLP_DIM, HIDDEN_SIZE // BLOCK_SIZE), dtype=jnp.float32) * 0.1 + 0.001
        down_W_packed = jax.random.randint(ks[5], (HIDDEN_SIZE, MLP_DIM // 2), 0, 64, dtype=jnp.int32)
        down_scales = jax.random.uniform(ks[6], (HIDDEN_SIZE, MLP_DIM // BLOCK_SIZE), dtype=jnp.float32) * 0.1 + 0.001
        return {'x': x, 'gate_W_packed': gate_W_packed, 'gate_scales': gate_scales, 'up_W_packed': up_W_packed, 'up_scales': up_scales, 'down_W_packed': down_W_packed, 'down_scales': down_scales}
    _L0_ffn_all = _L0_ffn_setup()
    _L0_ffn_in = {k: v for k, v in _L0_ffn_all.items() if k in ('gate_W_packed', 'gate_scales', 'up_W_packed', 'up_scales', 'down_W_packed', 'down_scales')}
    del _L0_ffn_all
    return {'x': x, 'ctx_1024': ctx_1024, 'L0_xattn_Wq': _L0_xattn_in['Wq'], 'L0_xattn_Wk': _L0_xattn_in['Wk'], 'L0_xattn_Wv': _L0_xattn_in['Wv'], 'L0_xattn_Wo': _L0_xattn_in['Wo'], 'L0_xattn_gq': _L0_xattn_in['gq'], 'L0_xattn_gk': _L0_xattn_in['gk'], 'L0_ffn_gate_W_packed': _L0_ffn_in['gate_W_packed'], 'L0_ffn_gate_scales': _L0_ffn_in['gate_scales'], 'L0_ffn_up_W_packed': _L0_ffn_in['up_W_packed'], 'L0_ffn_up_scales': _L0_ffn_in['up_scales'], 'L0_ffn_down_W_packed': _L0_ffn_in['down_W_packed'], 'L0_ffn_down_scales': _L0_ffn_in['down_scales']}

def reference(x, ctx_1024, L0_xattn_Wq, L0_xattn_Wk, L0_xattn_Wv, L0_xattn_Wo, L0_xattn_gq, L0_xattn_gk, L0_ffn_gate_W_packed, L0_ffn_gate_scales, L0_ffn_up_W_packed, L0_ffn_up_scales, L0_ffn_down_W_packed, L0_ffn_down_scales):
    import jax
    import jax.numpy as jnp

    def _L0_xattn_ref(hidden_states, encoder_hidden_states, Wq, Wk, Wv, Wo, gq, gk):
        import jax, jax.numpy as jnp
        import numpy as np
        EPS = 1e-05

        def rmsnorm(x, g, eps=EPS):
            var = jnp.mean(jnp.square(x), axis=-1, keepdims=True)
            return x * jax.lax.rsqrt(var + eps) * g
        B, Sq, _ = hidden_states.shape
        Skv = encoder_hidden_states.shape[1]
        D = gq.shape[0]
        H = Wq.shape[1] // D
        scale = 1.0 / np.sqrt(D)
        q = (hidden_states @ Wq).reshape(B, Sq, H, D)
        k = (encoder_hidden_states @ Wk).reshape(B, Skv, H, D)
        v = (encoder_hidden_states @ Wv).reshape(B, Skv, H, D)
        q = rmsnorm(q, gq)
        k = rmsnorm(k, gk)
        scores = jnp.einsum('bqhd,bkhd->bhqk', q, k) * scale
        attn = jax.nn.softmax(scores, axis=-1)
        out = jnp.einsum('bhqk,bkhd->bqhd', attn, v)
        out = out.reshape(B, Sq, H * D)
        return out @ Wo

    def _L0_ffn_ref(x, gate_W_packed, gate_scales, up_W_packed, up_scales, down_W_packed, down_scales):
        import jax, jax.numpy as jnp
        import numpy as np
        BLOCK_SIZE = 32
        HIDDEN_SIZE = 512
        MLP_DIM = 4096
        NVFP4_LUT = jnp.array([0.0, 0.5, 1.0, 1.5, 2.0, 3.0, 4.0, 6.0, 0.0, -0.5, -1.0, -1.5, -2.0, -3.0, -4.0, -6.0], dtype=jnp.float32)

        def dequant_nvfp4(W_packed, scales, block=BLOCK_SIZE):
            N = W_packed.shape[0]
            low = W_packed & 15
            high = W_packed >> 4 & 15
            idx = jnp.stack([low, high], axis=-1).reshape(N, -1)
            vals = NVFP4_LUT[idx]
            K = vals.shape[1]
            vals = vals.reshape(N, K // block, block) * scales[:, :, None]
            return vals.reshape(N, K)
        B, S, H = x.shape
        xt = x.reshape(B * S, H)
        Wg = dequant_nvfp4(gate_W_packed, gate_scales)
        Wu = dequant_nvfp4(up_W_packed, up_scales)
        Wd = dequant_nvfp4(down_W_packed, down_scales)
        gate = jnp.einsum('th,nh->tn', xt, Wg)
        up = jnp.einsum('th,nh->tn', xt, Wu)
        gelu = jnp.tanh(0.7978845608028654 * (gate + 0.044715 * gate ** 3)) * gate * 0.5 + gate * 0.5
        inter = gelu * up
        out = jnp.einsum('tn,hn->th', inter, Wd)
        return out.reshape(B, S, H)
    x = x + _L0_xattn_ref(_layernorm(x, axis=-1), ctx_1024, L0_xattn_Wq, L0_xattn_Wk, L0_xattn_Wv, L0_xattn_Wo, L0_xattn_gq, L0_xattn_gk)
    x = x + _L0_ffn_ref(_layernorm(x, axis=-1), L0_ffn_gate_W_packed, L0_ffn_gate_scales, L0_ffn_up_W_packed, L0_ffn_up_scales, L0_ffn_down_W_packed, L0_ffn_down_scales)
    return x

_drawn_inputs = setup_inputs


def setup_inputs(seed=0):
    import zlib

    import numpy as np

    out = dict(_drawn_inputs(seed))
    spreads = {'L0_xattn_gq': (1.0, 0.2), 'L0_xattn_gk': (1.0, 0.2)}
    factors = {}
    for name, (base, spread) in spreads.items():
        noise = np.random.default_rng([zlib.crc32(name.encode()), seed]).standard_normal(out[name].shape)
        drawn = base * np.exp(spread * noise) if base else spread * noise
        out[name] = jnp.asarray(drawn.astype(out[name].dtype))
    for name, factor in factors.items():
        out[name] = (out[name] * factor).astype(out[name].dtype)
    return out
```

```python
from contextlib import ExitStack

import numpy as np

import concourse.bass as bass
import concourse.mybir as mybir

F32 = mybir.dt.float32
F32R = mybir.dt.float32r
BF16 = mybir.dt.bfloat16
I32 = mybir.dt.int32
I16 = mybir.dt.int16
ALU = mybir.AluOpType
ACT = mybir.ActivationFunctionType
AX_X = mybir.AxisListType.X

P = 128
BATCH, SQ, DIM = 16, 100, 512
SKV, CDIM = 361, 256
HEADS, HD = 16, 128
MLP = 4096
FP4_BLOCK = 32
EPS = 1e-5
TOKENS = BATCH * SQ
BANK = 512
NBANKS = 8

GB = 4
NG = BATCH // GB
GT = GB * SQ
QH = 4
NQUAD = HEADS // QH
DC = DIM // P
CC = CDIM // P
KT = 3
KP = 122
KPAD = KT * KP
SCOLS = SKV + SKV % 2
LASTK = SKV - (KT - 1) * KP
UNITS = NG * NQUAD * GB

JT = MLP // (2 * P)
NCHUNK = 4
CT = TOKENS // NCHUNK
GELU_C = 0.7978845608028654
GELU_A = 0.044715


class Counter:

    def __init__(self, sem):
        self.sem, self.value = sem, 0

    def after(self, step):
        self.value += step
        return (self, self.value)

    def mark(self):
        return (self, self.value)


class Queue:

    def __init__(self):
        self.steps, self.seen = [], {}

    def wait(self, *marks):
        for counter, value in marks:
            if self.seen.get(counter, 0) < value:
                self.seen[counter] = value
                self.steps.append(lambda e, s=counter.sem, v=value: e.wait_ge(s, v))

    def do(self, emit, counter=None, step=1):
        if counter is None:
            self.steps.append(emit)
            return None
        self.steps.append(lambda e: emit(e).then_inc(counter.sem, step))
        return counter.after(step)

    def replay(self, engine):
        for s in self.steps:
            s(engine)


class Place:

    def __init__(self, t):
        self.t, self.last_use = t, []


class Turns:

    def __init__(self, tensors):
        self.places, self.n = [Place(t) for t in tensors], 0

    def next(self):
        self.n += 1
        return self.places[(self.n - 1) % len(self.places)]


class Builder:
    def __init__(self, nc, ctx, d):
        self.nc, self.ctx, self.d = nc, ctx, d
        self.pe, self.act, self.dve, self.pool, self.sp = (Queue() for _ in range(5))
        self.banks = Turns([ctx.enter_context(nc.psum_tensor(f"bank{i}", [P, BANK], F32)) for i in range(NBANKS)])
        self.counters = {}

    def count(self, name):
        if name not in self.counters:
            self.counters[name] = Counter(self.ctx.enter_context(self.nc.semaphore(name)))
        return self.counters[name]

    def sb(self, stack, name, shape, dt=F32):
        return stack.enter_context(self.nc.sbuf_tensor(name, shape, dt))

    def matmul3(self, out, terms, counter):
        passes = [ab for lh, ll, rh, rl in terms for ab in ((lh, rh), (lh, rl), (ll, rh))]
        for i, (a, b) in enumerate(passes):
            first, last = i == 0, i == len(passes) - 1
            mark = self.pe.do(lambda e, a=a, b=b, f=first, l=last: e.matmul(out, a, b, start=f, stop=l),
                              counter if last else None)
        return mark

    def split(self, hi, lo, src, hi_engine, lo_engine, name, ready):
        hi_engine.wait(*ready)
        if hi_engine is self.act:
            m_hi = hi_engine.do(lambda e: e.copy(hi, src), self.count(name + "_hi"))
        else:
            m_hi = hi_engine.do(lambda e: e.tensor_scalar(hi, src, 1.0, 1.0, ALU.mult, ALU.mult),
                                self.count(name + "_hi"))
        lo_engine.wait(*ready, m_hi)
        m_lo = lo_engine.do(lambda e: e.tensor_tensor(lo, src, hi.bitcast(F32), ALU.subtract),
                            self.count(name + "_lo"))
        return [m_hi, m_lo]

    def load(self, dst, src, name, queue=None):
        return (queue or self.sp).do(lambda e: e.dma_start(dst, src), self.count(name), 16)


def build_constants(b, s):
    nc, d = b.nc, b.d
    b.ident = b.sb(s, "ident", [P, P])
    b.power = b.sb(s, "power", [P, QH * GB])
    b.selector_f = b.sb(s, "selector_f", [P, P])
    b.selector = b.sb(s, "selector", [P, QH, P], F32R)
    m = b.pool.do(lambda e: e.memset(b.ident[:, :], 0.0), b.count("s_const"))
    b.pool.wait(m)
    b.const = [b.pool.do(lambda e: e.affine_select(out=b.ident[:, :], in_=b.ident[:, :], compare_op=ALU.not_equal,
                                                   fill=1.0, base=0, pattern=[[-1, P]], channel_multiplier=1),
                         b.count("s_const"))]
    b.const.append(b.pool.do(lambda e: e.memset(b.power[:, :], -0.5), b.count("s_const")))
    m = b.pool.do(lambda e: e.memset(b.selector_f[:, :], 0.0), b.count("s_const"))
    for h in range(QH):
        b.pool.wait(m)
        b.pool.do(lambda e, h=h: e.memset(b.selector_f[:, h:h + 1], 1.0), b.count("s_const"))
        b.pool.wait(b.count("s_const").mark())
        m = b.pool.do(lambda e, h=h: e.tensor_copy(b.selector[:, h, :], b.selector_f[:, :]), b.count("s_const"))
        b.pool.wait(m)
        m = b.pool.do(lambda e, h=h: e.memset(b.selector_f[:, h:h + 1], 0.0), b.count("s_const"))
    b.const.append(m)


class Attention:
    def __init__(self, b, s):
        self.b = b
        sb = lambda name, shape, dt=F32: b.sb(s, name, shape, dt)
        pair = lambda name, shape: (sb(name + "_hi", shape, F32R), sb(name + "_lo", shape, F32R))
        self.ctxT = [pair(f"ctxT{i}", [P, CC, KPAD]) for i in range(GB)]
        self.ctxN = [pair(f"ctxN{i}", [KP, KT, CDIM]) for i in range(GB)]
        self.ctx_ready, self.ctx_used = [[] for _ in range(GB)], [[] for _ in range(GB)]
        self.ctxT_raw = Place(sb("ctxT_raw", [P, CC, KPAD]))
        self.ctxN_raw = Place(sb("ctxN_raw", [KP, KT, CDIM]))
        self.wk, self.wk_raw = pair("wk", [P, CC, QH * HD]), Place(sb("wk_raw", [P, CC, QH * HD]))
        self.wk_used = []
        self.head_w = Turns([pair(f"head_w{i}", [P, DIM]) for i in range(3)])
        self.head_raw = Turns([sb(f"head_raw{i}", [P, DIM]) for i in range(2)])
        self.wv_ring = Turns([pair(f"wv{i}", [P, CC * HD]) for i in range(2)])
        self.wv_raw = Turns([sb(f"wv_raw{i}", [P, CC * HD]) for i in range(2)])
        self.gqk = sb("gqk", [P, 3])
        self.xlnT = pair("xlnT", [P, DC, GT])
        self.xlnT_used, self.xlnT_ready = [], []
        self.qT = [pair(f"qT{h}", [P, GT]) for h in range(QH)]
        self.qT_used, self.qT_ready = [[] for _ in range(QH)], [[] for _ in range(QH)]
        self.q_sq = Place(sb("q_sq", [P, GT]))
        self.q_sq_split = Turns([pair(f"q_sq{i}", [P, GT]) for i in range(2)])
        self.q_var = Place(sb("q_var", [QH, GT]))
        self.q_rstd = Turns([sb(f"q_rstd{i}", [SQ, GB * QH]) for i in range(2)])
        self.k_sq = Turns([sb(f"k_sq{i}", [KP, QH * HD]) for i in range(1)])
        self.k_ss = Turns([sb(f"k_ss{i}", [KP, KT * QH]) for i in range(2)])
        self.khat = Place(sb("khat", [KP, KT, QH * HD]))
        self.kT = [pair(f"kT{h}", [P, KPAD]) for h in range(QH)]
        self.kT_used, self.kT_ready = [[] for _ in range(QH)], [[] for _ in range(QH)]
        self.attn = [Place(sb(f"attn{h}", [SQ, KPAD])) for h in range(QH)]
        self.stats = Turns([sb(f"stats{i}", [SQ, 3 * QH]) for i in range(2)])
        self.aT = pair("aT", [KP, KT, QH * SQ])
        self.aT_used, self.aT_ready = [], []
        self.yT = pair("yT", [P, CC, QH, GT])
        self.yT_used, self.yT_ready = [], []
        self.oT = Turns([pair(f"oT{i}", [P, GT]) for i in range(2)])
        self.x_raw = Place(sb("x_raw", [SQ, DIM]))
        self.x_norm = Place(sb("x_norm", [SQ, DIM]))
        self.ln_small = Turns([sb(f"ln_small{i}", [SQ, 12]) for i in range(2)])
        self.x1T = Place(sb("x1T", [P, DC, GT]))
        self.x1T_done = []
        self.x2T = Place(sb("x2T", [P, DC * SQ]))
        self.head_queue, self.wv_queue = [], []
        self.spilled = []

    def setup(self):
        b = self.b
        m = [b.load(self.gqk[:, 0:1], b.d["gq"], "d_gq"), b.load(self.gqk[:, 1:2], b.d["gk"], "d_gk")]
        b.dve.wait(*m)
        self.gqk_ready = b.dve.do(lambda e: e.scalar_tensor_tensor(
            out=self.gqk[:, 2:3], in0=self.gqk[:, 0:1], scalar=float(HD) ** -0.5, in1=self.gqk[:, 1:2],
            op0=ALU.mult, op1=ALU.mult), b.count("s_gqk"))
        self.pads = [b.dve.do(lambda e: e.memset(self.ctxT_raw.t[:, :, SKV:KPAD], 0.0), b.count("s_pad")),
                     b.dve.do(lambda e: e.memset(self.ctxN_raw.t[96:KP, KT - 1, :], 0.0), b.count("s_pad"))]
        for h in range(QH):
            self.pads.append(b.dve.do(lambda e, h=h: e.memset(self.attn[h].t[:, SKV:KPAD], 0.0), b.count("s_pad")))

    def load_ctx(self, batch):
        b, i = self.b, batch % GB
        b.sp.wait(*self.pads, *self.ctxT_raw.last_use, *self.ctxN_raw.last_use)
        mT = b.load(self.ctxT_raw.t[:, :, 0:SKV], b.d["ctxT"][batch], "d_ctxT")
        mN = [b.load(self.ctxN_raw.t[:, 0:KT - 1, :],
                     b.d["ctx"][batch, 0:(KT - 1) * KP, :].rearrange("(t p) c -> p t c", p=KP), "d_ctxN"),
              b.load(self.ctxN_raw.t[0:LASTK, KT - 1, :], b.d["ctx"][batch, (KT - 1) * KP:SKV, :], "d_ctxN2")]
        b.pool.wait(*self.ctx_used[i])
        (th, tl), (nh, nl) = self.ctxT[i], self.ctxN[i]
        mT = b.split(th[:, :, :], tl[:, :, :], self.ctxT_raw.t[:, :, :], b.pool, b.pool, "s_ctxT", [mT])
        mN = b.split(nh[:, :, :], nl[:, :, :], self.ctxN_raw.t[:, :, :], b.pool, b.pool, "s_ctxN", mN)
        self.ctxT_raw.last_use, self.ctxN_raw.last_use = mT, mN
        self.ctx_ready[i], self.ctx_used[i] = mT + mN, []

    def load_wk(self, quad):
        b = self.b
        b.sp.wait(*self.wk_raw.last_use)
        src = b.d["Wk"][:, quad * QH * HD:(quad + 1) * QH * HD].rearrange("(c p) n -> p c n", p=P)
        m = b.load(self.wk_raw.t[:, :, :], src, "d_wk")
        b.pool.wait(*self.wk_used)
        self.wk_used = []
        self.wk_ready = b.split(self.wk[0][:, :, :], self.wk[1][:, :, :], self.wk_raw.t[:, :, :],
                                b.pool, b.pool, "s_wk", [m])
        self.wk_raw.last_use = self.wk_ready

    def load_head_weight(self, kind, head):
        b = self.b
        raw = self.head_raw.next()
        b.sp.wait(*raw.last_use)
        if kind == "q":
            src = b.d["Wq"][:, head * HD:(head + 1) * HD].rearrange("(c p) n -> p c n", p=P)
            dst = raw.t[:, :].rearrange("p (c n) -> p c n", c=DC)
        else:
            src, dst = b.d["Wo"][head * HD:(head + 1) * HD, :], raw.t[:, :]
        m = b.load(dst, src, f"d_head{self.head_raw.n % 2}")
        slot = self.head_w.next()
        b.pool.wait(*slot.last_use)
        raw.last_use = b.split(slot.t[0][:, :], slot.t[1][:, :], raw.t[:, :], b.pool, b.pool, "s_headw", [m])
        self.head_queue.append((slot, raw.last_use))

    def load_wv(self, head):
        b = self.b
        raw = self.wv_raw.next()
        b.sp.wait(*raw.last_use)
        src = b.d["Wv"][:, head * HD:(head + 1) * HD].rearrange("(c p) n -> p c n", p=P)
        m = b.load(raw.t[:, :].rearrange("p (c n) -> p c n", c=CC), src, f"d_wv{self.wv_raw.n % 2}")
        slot = self.wv_ring.next()
        b.pool.wait(*slot.last_use)
        raw.last_use = b.split(slot.t[0][:, :], slot.t[1][:, :], raw.t[:, :], b.pool, b.pool, "s_wv", [m])
        self.wv_queue.append((slot, raw.last_use))

    def layernorm(self, src, ready):
        b = self.b
        small, norm = self.ln_small.next(), self.x_norm
        st = small.t
        b.dve.wait(*small.last_use, *ready)
        m = b.dve.do(lambda e: e.bn_stats(st[:, 0:6], src), b.count("s_bn"))
        b.dve.wait(m)
        m = b.dve.do(lambda e: e.bn_aggr(st[:, 6:8], st[:, 0:6]), b.count("s_bn"))
        b.dve.wait(m)
        m = b.dve.do(lambda e: e.tensor_scalar(st[:, 8:9], st[:, 7:8], EPS, None, ALU.add), b.count("s_bn"))
        b.pool.wait(m, *b.const)
        m = b.pool.do(lambda e: e.tensor_tensor(st[:, 9:10], st[:, 8:9], b.power[0:SQ, 0:1], ALU.pow),
                      b.count("s_lnrstd"))
        b.dve.wait(m, *norm.last_use)
        m = b.dve.do(lambda e: e.tensor_scalar(norm.t[:, :], src, st[:, 6:7], st[:, 9:10], ALU.subtract, ALU.mult),
                     b.count("s_xnorm"))
        small.last_use = [m]
        return m

    def norm_transposed(self, ready, parity):
        b, norm = self.b, self.x_norm
        bank = b.banks.next()
        b.pe.wait(*bank.last_use)
        b.pe.wait(ready, *b.const)
        for c in range(DC):
            if parity:
                lo = (c // 2) * 2 * P + c % 2
                src = norm.t[:, lo:lo + 2 * P - 1:2]
            else:
                src = norm.t[:, c * P:(c + 1) * P]
            m = b.pe.do(lambda e, c=c, src=src: e.transpose(bank.t[:, c * SQ:(c + 1) * SQ], src, b.ident[0:SQ, 0:SQ]),
                        b.count("s_normT") if c == DC - 1 else None)
        norm.last_use = [m]
        return bank, m

    def ln1(self, batch):
        b, i = self.b, batch % GB
        b.sp.wait(*self.x_raw.last_use)
        m = b.load(self.x_raw.t[:, :], b.d["x"][batch], "d_x")
        m = self.layernorm(self.x_raw.t[:, :], [m])
        self.x_raw.last_use = [m]
        bank, m = self.norm_transposed(m, False)
        if i == 0:
            b.act.wait(*self.xlnT_used)
            b.dve.wait(*self.xlnT_used)
            self.xlnT_used, self.xlnT_ready = [], []
        cols = slice(i * SQ, (i + 1) * SQ)
        bank.last_use = b.split(self.xlnT[0][:, :, cols], self.xlnT[1][:, :, cols],
                               bank.t[:, 0:DC * SQ].rearrange("p (c n) -> p c n", c=DC), b.act, b.dve, "s_xlnT", [m])
        self.xlnT_ready += bank.last_use

    def queries(self, loads):
        b = self.b
        xh, xl = self.xlnT
        sbank = b.banks.next()
        b.pe.wait(*sbank.last_use)
        ssum = sbank.t[:, 0:GT]
        squares = []

        def add_squares(h):
            place, ready = squares[h]
            b.pe.wait(*ready, *b.const)
            for k in range(2):
                m = b.pe.do(lambda e, k=k: e.matmul(ssum, b.selector[:, h, :], place.t[k][:, :],
                                                    start=h == 0 and k == 0, stop=h == QH - 1 and k == 1),
                            b.count("s_qss") if k else None)
            place.last_use = [m]
            return m

        for h in range(QH):
            slot, wready = self.head_queue.pop(0)
            wh, wl = slot.t
            bank = b.banks.next()
            b.pe.wait(*bank.last_use)
            b.pe.wait(*wready, *self.xlnT_ready)
            q = bank.t[:, 0:GT]
            m = b.matmul3(q, [(wh[:, c * HD:(c + 1) * HD], wl[:, c * HD:(c + 1) * HD], xh[:, c, :], xl[:, c, :])
                              for c in range(DC)], b.count("s_q"))
            slot.last_use = self.xlnT_used = [m]
            b.act.wait(m, *self.q_sq.last_use)
            m2 = b.act.do(lambda e, q=q: e.activation(self.q_sq.t[:, :], q, ACT.Square), b.count("s_qsq"))
            b.act.wait(*self.qT_used[h], self.gqk_ready)
            b.dve.wait(*self.qT_used[h])
            qh, ql = self.qT[h]
            m3 = b.act.do(lambda e, q=q, o=qh: e.activation(o[:, :], q, ACT.Copy, scale=self.gqk[:, 2:3]), b.count("s_qT_hi"))
            b.dve.wait(m3)
            m4 = b.dve.do(lambda e, q=q, o=ql, hi=qh: e.scalar_tensor_tensor(
                out=o[:, :], in0=q, scalar=self.gqk[:, 2:3], in1=hi[:, :].bitcast(F32), op0=ALU.mult, op1=ALU.subtract),
                b.count("s_qT_lo"))
            bank.last_use = [m2, m4]
            self.qT_ready[h], self.qT_used[h] = [m3, m4], []
            place = self.q_sq_split.next()
            b.act.wait(*place.last_use)
            b.dve.wait(*place.last_use)
            sh, sl = place.t
            self.q_sq.last_use = b.split(sh[:, :], sl[:, :], self.q_sq.t[:, :], b.act, b.dve, "s_qsqs", [m2])
            squares.append((place, self.q_sq.last_use))
            if h > 0:
                add_squares(h - 1)
            self.load_head_weight(*loads[h])
        m = add_squares(QH - 1)
        b.dve.wait(m, *self.q_var.last_use)
        m = b.dve.do(lambda e: e.tensor_scalar(self.q_var.t[:, :], ssum[0:QH, :], 1.0 / HD, EPS, ALU.mult, ALU.add),
                     b.count("s_qvar"))
        sbank.last_use = [m]
        bank = b.banks.next()
        b.pe.wait(*bank.last_use)
        b.pe.wait(m)
        for i in range(GB):
            m = b.pe.do(lambda e, i=i: e.transpose(bank.t[0:SQ, i * QH:(i + 1) * QH], self.q_var.t[:, i * SQ:(i + 1) * SQ],
                                                   b.ident[0:QH, 0:QH]), b.count("s_qvarT") if i == GB - 1 else None)
        self.q_var.last_use = [m]
        rstd = self.q_rstd.next()
        b.dve.wait(m, *rstd.last_use)
        m = b.dve.do(lambda e: e.tensor_copy(rstd.t[:, :], bank.t[0:SQ, 0:GB * QH]), b.count("s_qvarT_sb"))
        bank.last_use = [m]
        b.pool.wait(m, *b.const)
        m = b.pool.do(lambda e: e.tensor_tensor(rstd.t[:, :], rstd.t[:, :], b.power[0:SQ, 0:GB * QH], ALU.pow),
                      b.count("s_qrstd"))
        self.rstd_q, self.rstd_q_ready = rstd, m

    def keys(self, unit):
        b, i = self.b, unit % GB
        th, tl = self.ctxT[i]
        wh, wl = self.wk
        ss = self.k_ss.next()
        b.dve.wait(*ss.last_use)
        self.k_banks, marks = [], []
        b.pe.wait(*self.ctx_ready[i], *self.wk_ready)
        for t in range(KT):
            bank = b.banks.next()
            b.pe.wait(*bank.last_use)
            ks = slice(t * KP, (t + 1) * KP)
            m = b.matmul3(bank.t[0:KP, :], [(th[:, c, ks], tl[:, c, ks], wh[:, c, :], wl[:, c, :]) for c in range(CC)],
                          b.count("s_k"))
            sq = self.k_sq.next()
            b.act.wait(*sq.last_use)
            b.act.wait(m)
            m2 = b.act.do(lambda e, s=sq, k=bank: e.activation(s.t[:, :], k.t[0:KP, :], ACT.Square), b.count("s_ksq"))
            b.dve.wait(m2)
            m3 = b.dve.do(lambda e, s=sq, t=t: e.tensor_reduce(
                ss.t[:, t * QH:(t + 1) * QH], s.t[:, :].rearrange("p (h d) -> p h d", h=QH), AX_X, ALU.add),
                b.count("s_kss"))
            sq.last_use = [m3]
            self.k_banks.append(bank)
        self.wk_used = [m]
        self.ctx_used[i] = [m]
        b.pool.wait(m3, *b.const)
        m4 = b.pool.do(lambda e: e.tensor_scalar(ss.t[:, :], ss.t[:, :], 1.0 / HD, EPS, ALU.mult, ALU.add), b.count("s_kvar"))
        b.pool.wait(m4)
        m5 = b.pool.do(lambda e: e.tensor_tensor(ss.t[:, :], ss.t[:, :], b.power[0:KP, 0:KT * QH], ALU.pow), b.count("s_krstd"))
        self.k_rstd = (ss, m5)

    def normalise_keys(self):
        b = self.b
        ss, m5 = self.k_rstd
        b.dve.wait(m5, *self.khat.last_use)
        self.khat_ready = []
        for t, bank in enumerate(self.k_banks):
            m = b.dve.do(lambda e, t=t, k=bank: e.tensor_tensor(
                self.khat.t[:, t, :].rearrange("p (h d) -> p h d", h=QH),
                k.t[0:KP, :].rearrange("p (h d) -> p h d", h=QH),
                ss.t[:, t * QH:(t + 1) * QH].unsqueeze(2).broadcast_to([KP, QH, HD]), ALU.mult), b.count("s_khat"))
            bank.last_use = [m]
            self.khat_ready.append(m)
        ss.last_use = [m]

    def transpose_keys(self, hs=range(QH)):
        b = self.b
        b.pe.wait(*self.khat_ready, *b.const)
        for h in hs:
            bank = b.banks.next()
            b.pe.wait(*bank.last_use)
            for t in range(KT):
                m = b.pe.do(lambda e, t=t, h=h, k=bank: e.transpose(
                    k.t[:, t * KP:(t + 1) * KP], self.khat.t[:, t, h * HD:(h + 1) * HD], b.ident[0:KP, 0:KP]),
                    b.count("s_kTp") if t == KT - 1 else None)
            b.act.wait(*self.kT_used[h])
            b.dve.wait(*self.kT_used[h])
            self.kT_used[h] = []
            kh, kl = self.kT[h]
            self.kT_ready[h] = b.split(kh[:, :], kl[:, :], bank.t[:, 0:KPAD], b.act, b.dve, "s_kT", [m])
            bank.last_use = self.kT_ready[h]
        self.khat.last_use = [m]

    def scores(self, unit):
        b, i = self.b, unit % GB
        st = self.stats.next()
        b.dve.wait(*st.last_use)
        neg, total, inv = (st.t[:, k * QH:(k + 1) * QH] for k in range(3))
        rq = self.rstd_q.t
        b.act.wait(*self.pads)
        exps = []
        for h in range(QH):
            bank = b.banks.next()
            b.pe.wait(*bank.last_use)
            qs = slice(i * SQ, (i + 1) * SQ)
            (qh, ql), (kh, kl) = self.qT[h], self.kT[h]
            b.pe.wait(*self.kT_ready[h], *self.qT_ready[h])
            m = b.matmul3(bank.t[0:SQ, 0:SCOLS], [(qh[:, qs], ql[:, qs], kh[:, 0:SCOLS], kl[:, 0:SCOLS])], b.count("s_sc"))
            self.kT_used[h], self.qT_used[h] = [m], [m]
            b.dve.wait(m)
            m2 = b.dve.do(lambda e, h=h, k=bank: e.tensor_reduce(neg[:, h:h + 1], k.t[0:SQ, 0:SKV], AX_X, ALU.max,
                                                                 negate=True), b.count("s_max"))
            col = slice(i * QH + h, i * QH + h + 1)
            b.dve.wait(m2, self.rstd_q_ready)
            m2 = b.dve.do(lambda e, h=h, col=col: e.tensor_tensor(neg[:, h:h + 1], neg[:, h:h + 1], rq[:, col], ALU.mult),
                          b.count("s_negmax"))
            b.act.wait(m2, *self.attn[h].last_use)
            m3 = b.act.do(lambda e, h=h, k=bank, col=col: e.activation(self.attn[h].t[:, 0:SKV], k.t[0:SQ, 0:SKV], ACT.Exp,
                                                              bias=neg[:, h:h + 1], scale=rq[:, col], accum_out=total[:, h:h + 1]),
                          b.count("s_exp"))
            bank.last_use = [m3]
            exps.append(m3)
        self.rstd_q.last_use = exps
        b.dve.wait(*exps)
        m4 = b.dve.do(lambda e: e.reciprocal(inv, total), b.count("s_inv"))
        b.pool.wait(m4)
        self.attn_ready = []
        for h in range(QH):
            self.attn_ready.append(b.pool.do(lambda e, h=h: e.tensor_scalar(
                self.attn[h].t[:, 0:SKV], self.attn[h].t[:, 0:SKV], inv[:, h:h + 1], 1.0, ALU.mult, ALU.mult),
                b.count("s_attn")))
        st.last_use = [self.attn_ready[-1]]

    def transpose_attn(self):
        b = self.b
        ah, al = self.aT
        b.act.wait(*self.aT_used)
        b.dve.wait(*self.aT_used)
        self.aT_used, self.aT_ready = [], []
        for h in range(QH):
            bank = b.banks.next()
            b.pe.wait(*bank.last_use)
            b.pe.wait(self.attn_ready[h])
            for t in range(KT):
                m = b.pe.do(lambda e, t=t, h=h, k=bank: e.transpose(
                    k.t[0:KP, t * SQ:(t + 1) * SQ], self.attn[h].t[:, t * KP:(t + 1) * KP], b.ident[0:SQ, 0:SQ]),
                    b.count("s_aTp") if t == KT - 1 else None)
            self.attn[h].last_use = [m]
            hs = slice(h * SQ, (h + 1) * SQ)
            bank.last_use = b.split(ah[:, :, hs], al[:, :, hs], bank.t[0:KP, 0:KT * SQ].rearrange("p (t n) -> p t n", t=KT),
                                   b.act, b.dve, "s_aT", [m])
            self.aT_ready += bank.last_use

    def attend(self, unit):
        b, i = self.b, unit % GB
        (ah, al), (nh, nl), (yh, yl) = self.aT, self.ctxN[i], self.yT
        b.pe.wait(*self.aT_ready)
        if i == 0:
            b.act.wait(*self.yT_used)
            b.dve.wait(*self.yT_used)
            self.yT_used, self.yT_ready = [], []
        for c in range(CC):
            bank = b.banks.next()
            b.pe.wait(*bank.last_use)
            cs = slice(c * P, (c + 1) * P)
            m = b.matmul3(bank.t[:, 0:QH * SQ], [(nh[:, t, cs], nl[:, t, cs], ah[:, t, :], al[:, t, :]) for t in range(KT)],
                          b.count("s_y"))
            qs = slice(i * SQ, (i + 1) * SQ)
            bank.last_use = b.split(yh[:, c, :, qs], yl[:, c, :, qs],
                                   bank.t[:, 0:QH * SQ].rearrange("p (h n) -> p h n", h=QH), b.act, b.dve, "s_yT", [m])
            self.yT_ready += bank.last_use
        self.aT_used = [m]
        self.ctx_used[i] = self.ctx_used[i] + [m]

    def project(self, group, quad, ahead):
        b = self.b
        if quad == 0:
            b.sp.wait(*self.x1T.last_use)
            m = b.load(self.x1T.t[:, :, :], b.d["xT"][:, :, group * GT:(group + 1) * GT], "d_xT")
            self.x1T_done = [m]
        yh, yl = self.yT
        heads = []

        def value(h):
            slot, wready = self.wv_queue.pop(0)
            wh, wl = slot.t
            bank = b.banks.next()
            b.pe.wait(*bank.last_use)
            b.pe.wait(*wready, *self.yT_ready)
            m = b.matmul3(bank.t[:, 0:GT], [(wh[:, c * HD:(c + 1) * HD], wl[:, c * HD:(c + 1) * HD],
                                             yh[:, c, h, :], yl[:, c, h, :]) for c in range(CC)], b.count("s_o"))
            slot.last_use = [m]
            self.yT_used = [m]
            o = self.oT.next()
            b.act.wait(*o.last_use)
            b.dve.wait(*o.last_use)
            bank.last_use = b.split(o.t[0][:, :], o.t[1][:, :], bank.t[:, 0:GT], b.act, b.dve, "s_oT", [m])
            heads.append((o, bank.last_use))
            if h + 2 < QH:
                self.load_wv(quad * QH + h + 2)

        value(0)
        value(1)
        outs = [b.banks.next() for _ in range(DC)]
        for bank in outs:
            b.pe.wait(*bank.last_use)
        for h in range(QH):
            slot, wready = self.head_queue.pop(0)
            wh, wl = slot.t
            o, oready = heads[h]
            b.pe.wait(*wready, *oready)
            for c in range(DC):
                cs = slice(c * P, (c + 1) * P)
                out = outs[c].t[:, 0:GT]
                for k, (a, r) in enumerate(((wh, o.t[0]), (wh, o.t[1]), (wl, o.t[0]))):
                    f, l = h == 0 and k == 0, h == QH - 1 and k == 2
                    m = b.pe.do(lambda e, out=out, a=a, r=r, cs=cs, f=f, l=l: e.matmul(
                        out, a[:, cs], r[:, :], start=f, stop=l),
                        b.count("s_out") if k == 2 and (c == DC - 1 or h == QH - 1) else None)
                if h == QH - 1:
                    b.dve.wait(m, *self.x1T_done)
                    md = b.dve.do(lambda e, c=c, out=out: e.tensor_tensor(self.x1T.t[:, c, :], out, self.x1T.t[:, c, :],
                                                                          ALU.add), b.count("s_x1T"))
                    outs[c].last_use = [md]
            slot.last_use = [m]
            o.last_use = [m]
            if h + 2 < QH:
                value(h + 2)
            if ahead:
                self.load_head_weight(*ahead.pop(0))
        self.x1T_done = [md]

    def ln2(self, group):
        b = self.b
        gs = slice(group * GT, (group + 1) * GT)
        b.sp.wait(*self.x1T_done)
        store = b.sp.do(lambda e: e.dma_start(b.d["x1T"][:, :, gs], self.x1T.t[:, :, :]), b.count("d_x1T_out"), 16)
        self.spilled.append(store)
        for j in range(GB):
            bank = b.banks.next()
            b.pe.wait(*bank.last_use)
            b.pe.wait(*self.x1T_done)
            for c in range(DC):
                m = b.pe.do(lambda e, c=c, j=j, k=bank: e.transpose(
                    k.t[0:SQ, c * P:(c + 1) * P], self.x1T.t[:, c, j * SQ:(j + 1) * SQ], b.ident[:, :]),
                    b.count("s_x1") if c == DC - 1 else None)
            mt = m
            m = self.layernorm(bank.t[0:SQ, :], [m])
            bank.last_use = [m]
            nbank, m = self.norm_transposed(m, True)
            b.act.wait(m, *self.x2T.last_use)
            m = b.act.do(lambda e, k=nbank: e.copy(self.x2T.t[:, :], k.t[:, 0:DC * SQ]), b.count("s_x2T"))
            nbank.last_use = [m]
            b.sp.wait(m)
            cols = slice(group * GT + j * SQ, group * GT + (j + 1) * SQ)
            m = b.sp.do(lambda e, cols=cols: e.dma_start(b.d["x2T"][:, :, cols],
                                                         self.x2T.t[:, :].rearrange("p (c n) -> p c n", c=DC)),
                        b.count("d_x2T_out"), 16)
            self.x2T.last_use = [m]
            self.spilled.append(m)
        self.x1T.last_use = [mt, store]

    def run(self):
        b = self.b
        self.setup()
        self.load_ctx(0)
        self.load_wk(0)
        for h in range(3):
            self.load_head_weight("q", h)
        for i in range(GB):
            self.ln1(i)
        self.load_ctx(1)
        self.keys(0)
        self.normalise_keys()
        self.queries([("q", 3 + h) for h in range(QH)])
        self.load_ctx(2)
        self.load_ctx(3)
        pending = None
        for u in range(UNITS + 1):
            group, quad, i = u // (NQUAD * GB), u // GB % NQUAD, u % GB
            lastq = quad == NQUAD - 1
            if u < UNITS:
                self.transpose_keys()
                if u + 1 < UNITS:
                    self.keys(u + 1)
                self.scores(u)
                if u + 1 < UNITS:
                    self.normalise_keys()
            if u > 0:
                self.attend(u - 1)
            if u < UNITS:
                self.transpose_attn()
            if pending is not None:
                g, q = pending
                nextq = g * NQUAD + q + 2
                ahead = [("o", q * QH + 3)]
                if nextq < NG * NQUAD:
                    ahead += [("q", nextq % NQUAD * QH + h) for h in range(3)]
                elif nextq == NG * NQUAD:
                    ahead += [("o", (q + 1) * QH + h) for h in range(3)]
                self.project(g, q, ahead)
                if q == NQUAD - 1:
                    self.ln2(g)
                pending = None
            if u >= UNITS:
                break
            qn = u // GB + 1
            if i == 2 and qn < NG * NQUAD:
                self.load_wk(qn % NQUAD)
            if i == 2:
                for h in range(2):
                    self.load_wv(quad * QH + h)
            if lastq and group + 1 < NG:
                if i == 0:
                    self.ln1((group + 1) * GB)
                    self.ln1((group + 1) * GB + 1)
                if i == 1:
                    self.ln1((group + 1) * GB + 2)
                    self.ln1((group + 1) * GB + 3)
                if i > 0:
                    self.load_ctx((group + 1) * GB + i - 1)
            if quad == 0 and group > 0 and i == 0:
                self.load_ctx(group * GB + GB - 1)
            if i == GB - 1:
                if qn < NG * NQUAD:
                    self.queries([("q", qn % NQUAD * QH + 3)] + [("o", quad * QH + h) for h in range(3)])
                pending = (group, quad)


class FeedForward:

    def __init__(self, b, s):
        self.b = b
        sb = lambda name, shape, dt=F32: b.sb(s, name, shape, dt)
        pair = lambda name, shape: (sb(name + "_hi", shape, F32R), sb(name + "_lo", shape, F32R))
        self.xT = pair("xT", [P, DC, TOKENS])
        self.x_raw = Turns([sb(f"xT_raw{i}", [P, DC, CT]) for i in range(2)])
        self.x_ready = []
        self.yT = sb("yT", [P, DC, TOKENS])
        self.y_done = [[] for _ in range(NCHUNK)]
        self.weights = [Turns([pair(f"{n}{i}", [P, 4 * 2 * P]) for i in range(2)]) for n in ("gate", "up", "down")]
        self.packed = [Turns([sb(f"{n}_packed{i}", [P, 4 * P], I32) for i in range(2)]) for n in ("gate", "up", "down")]
        self.scale = [Turns([sb(f"{n}_scale{i}", [P, 4 * P]) for i in range(2)]) for n in ("gate", "up", "down")]
        t16 = lambda name, dt: [Place(sb(f"{name}{i}", [P, 4 * P], dt)) for i in range(1)][0]
        self.mag, self.sign = t16("mag", I16), t16("sign", I16)
        self.over4, self.over6 = t16("over4", BF16), t16("over6", BF16)
        self.value = t16("value", BF16)
        self.wide = Turns([sb(f"wide{i}", [P, 4 * P]) for i in range(2)])
        self.sq = Turns([sb(f"sq{i}", [P, CT]) for i in range(2)])
        self.tanh = Turns([sb(f"tanh{i}", [P, CT]) for i in range(2)])
        self.act = Turns([sb(f"act{i}", [P, CT]) for i in range(2)])
        self.inter = Turns([pair(f"inter{i}", [P, CT]) for i in range(4)])

    def load_x(self, ch):
        b, cols = self.b, slice(ch * CT, (ch + 1) * CT)
        raw = self.x_raw.next()
        b.sp.wait(*raw.last_use)
        m = b.load(raw.t[:, :, :], b.d["x2T"][:, :, cols], f"d_x2T{ch % 2}")
        raw.last_use = b.split(self.xT[0][:, :, cols], self.xT[1][:, :, cols], raw.t[:, :, :], b.act, b.dve, "s_xT", [m])
        self.x_ready.append(raw.last_use)
        self.y_done[ch] = [b.load(self.yT[:, :, cols], b.d["x1T"][:, :, cols], f"d_yT{ch}")]

    def fetch(self, jt):
        b, self.fetched = self.b, []
        for k, name in enumerate(("gate", "up", "down")):
            packed, scale = self.packed[k].next(), self.scale[k].next()
            b.sp.wait(*packed.last_use, *scale.last_use)
            m = [b.load(packed.t[:, :], b.d[name + "_packed"][:, jt, :], f"d_{name}{jt % 2}"),
                 b.load(scale.t[:, :], b.d[name + "_scales"][:, jt, :].unsqueeze(1).broadcast_to([8, 16, 4 * P]),
                        f"d_{name}_s{jt % 2}")]
            self.fetched.append((packed, scale, m))

    def decode(self, k, nibble):
        b = self.b
        packed, scale, ready = self.fetched[k]
        if nibble == 0:
            slot = self.weights[k].next()
            b.act.wait(*slot.last_use)
            b.pool.wait(*slot.last_use)
            self.building[k] = (slot, [])
        slot, marks = self.building[k]
        codes = packed.t[:, :].bitcast(I16)[:, 0:8 * P:2]
        mag, sign, over4, over6, value = (x.t[:, :] for x in (self.mag, self.sign, self.over4, self.over6, self.value))
        c = b.count("s_decode")
        b.dve.wait(*ready)
        dve = lambda emit: b.dve.do(emit, c)
        dve(lambda e: e.tensor_scalar(sign, codes, 8 << 4 * nibble, 12 - 4 * nibble, ALU.bitwise_and,
                                      ALU.logical_shift_left))
        m = dve(lambda e: e.tensor_scalar(mag, codes, 4 * nibble, 7, ALU.logical_shift_right, ALU.bitwise_and))
        b.dve.wait(m)
        dve(lambda e: e.tensor_scalar(over4, mag, -4.0, 0.0, ALU.add, ALU.max))
        m = dve(lambda e: e.tensor_scalar(over6, mag, 7.0, 2.0, ALU.is_ge, ALU.mult))
        b.dve.wait(m)
        m = dve(lambda e: e.tensor_tensor(over4, over4, over6, ALU.add))
        b.dve.wait(m)
        m = dve(lambda e: e.tensor_tensor(value, over4, mag, ALU.add))
        b.dve.wait(m)
        m = dve(lambda e: e.tensor_tensor(value.bitcast(I16), value.bitcast(I16), sign, ALU.bitwise_or))
        wide = self.wide.next()
        b.dve.wait(*wide.last_use)
        b.dve.wait(m)
        m = dve(lambda e: e.scalar_tensor_tensor(out=wide.t[:, :], in0=value, scalar=0.5, in1=scale.t[:, :],
                                                 op0=ALU.mult, op1=ALU.mult))
        if k < 2:
            view = lambda t: t[:, :].rearrange("p (r z n) -> p r z n", r=2, z=2)[:, :, nibble, :]
            src = wide.t[:, :].rearrange("p (r n) -> p r n", r=2)
        else:
            view = lambda t: t[:, :].rearrange("p (z n) -> p z n", z=2)[:, nibble, :]
            src = wide.t[:, :]
        wide.last_use = b.split(view(slot.t[0]), view(slot.t[1]), src, b.act, b.pool, "s_weight", [m])
        marks += wide.last_use
        if nibble == 1:
            packed.last_use = scale.last_use = [m]

    def gate_up(self, ch):
        b = self.b
        cols = slice(ch * CT, (ch + 1) * CT)
        xh, xl = (t[:, :, cols] for t in self.xT)
        self.inters = []
        for z in range(2):
            psums = []
            for k, name in enumerate(("s_gate", "s_up")):
                slot, ready = self.current[k]
                wh, wl = (t[:, :].rearrange("p (c n) -> p c n", c=DC) for t in slot.t)
                bank = b.banks.next()
                b.pe.wait(*bank.last_use)
                b.pe.wait(*ready, *self.x_ready[ch])
                ns = slice(z * P, (z + 1) * P)
                m = b.matmul3(bank.t[:, 0:CT], [(wh[:, c, ns], wl[:, c, ns], xh[:, c, :], xl[:, c, :]) for c in range(DC)],
                              b.count(name))
                slot.last_use = [m]
                psums.append((bank, bank.t[:, 0:CT], m))
            (gbank, g, mg), (ubank, u, mu) = psums
            sq, th, ac = self.sq.next(), self.tanh.next(), self.act.next()
            b.act.wait(*sq.last_use, mg)
            m = b.act.do(lambda e, o=sq.t, g=g: e.activation(o[:, :], g, ACT.Square), b.count("s_g2"))
            b.dve.wait(m)
            m = b.dve.do(lambda e, o=sq.t: e.tensor_scalar(o[:, :], o[:, :], GELU_A * GELU_C, GELU_C, ALU.mult, ALU.add),
                         b.count("s_poly"))
            b.dve.wait(m)
            m = b.dve.do(lambda e, o=sq.t, g=g: e.tensor_tensor(o[:, :], g, o[:, :], ALU.mult), b.count("s_poly"))
            b.act.wait(*th.last_use, m)
            m = b.act.do(lambda e, o=th.t, i=sq.t: e.activation(o[:, :], i[:, :], ACT.Tanh), b.count("s_tanh"))
            sq.last_use = [m]
            b.dve.wait(*ac.last_use, m)
            m = b.dve.do(lambda e, o=ac.t, i=th.t, g=g: e.scalar_tensor_tensor(out=o[:, :], in0=i[:, :], scalar=1.0, in1=g,
                                                                              op0=ALU.add, op1=ALU.mult), b.count("s_gelu"))
            th.last_use = gbank.last_use = [m]
            b.dve.wait(m, mu)
            m = b.dve.do(lambda e, o=ac.t, u=u: e.scalar_tensor_tensor(out=o[:, :], in0=o[:, :], scalar=0.5, in1=u,
                                                                       op0=ALU.mult, op1=ALU.mult), b.count("s_inter"))
            ubank.last_use = [m]
            it = self.inter.next()
            b.act.wait(*it.last_use)
            b.pool.wait(*it.last_use)
            ac.last_use = b.split(it.t[0][:, :], it.t[1][:, :], ac.t[:, :], b.act, b.pool, "s_inters", [m])
            self.inters.append((it, ac.last_use))

    def down(self, ch, down, inters, last):
        b = self.b
        cols = slice(ch * CT, (ch + 1) * CT)
        slot, ready = down
        wh, wl = (t[:, :].rearrange("p (z n) -> p z n", z=2) for t in slot.t)
        b.pe.wait(*ready, *(m for _, r in inters for m in r))
        for c in range(DC):
            bank = b.banks.next()
            b.pe.wait(*bank.last_use)
            cs = slice(c * P, (c + 1) * P)
            m = b.matmul3(bank.t[:, 0:CT], [(wh[:, z, cs], wl[:, z, cs], inters[z][0].t[0][:, :], inters[z][0].t[1][:, :])
                                            for z in range(2)], b.count("s_down"))
            b.dve.wait(m, *self.y_done[ch])
            md = b.dve.do(lambda e, c=c, k=bank: e.tensor_tensor(self.yT[:, c, cols], k.t[:, 0:CT], self.yT[:, c, cols],
                                                                 ALU.add), b.count("s_yT_sum"))
            bank.last_use = [md]
        slot.last_use = [m]
        for it, _ in inters:
            it.last_use = [m]
        self.y_done[ch] = [md]
        if last:
            b.sp.wait(md)
            self.out_marks.append(b.sp.do(lambda e: e.dma_start(b.d["out"][:, :, cols], self.yT[:, :, cols]),
                                          b.count(f"d_out{ch}"), 16))

    def run(self):
        b = self.b
        self.out_marks, self.building = [], [None] * 3
        self.fetch(0)
        self.load_x(0)
        for k in range(3):
            for nibble in range(2):
                self.decode(k, nibble)
        for ch in range(1, NCHUNK):
            self.load_x(ch)
        pieces = [(k, n) for k in range(3) for n in range(2)]
        prev = None
        for jt in range(JT):
            self.current = list(self.building)
            todo = []
            for ch in range(NCHUNK):
                self.gate_up(ch)
                step = (ch, self.current[2], self.inters, jt == JT - 1)
                if prev:
                    self.down(*prev)
                prev = step
                if jt + 1 < JT:
                    if ch == 0:
                        self.fetch(jt + 1)
                        todo = list(pieces)
                    for _ in range((2, 2, 1, 1)[ch]):
                        self.decode(*todo.pop(0))
        self.down(*prev)
        b.sp.wait(*self.out_marks)


def build(nc, d):
    with ExitStack() as ctx:
        b = Builder(nc, ctx, d)
        build_constants(b, ctx)
        with ExitStack() as s:
            attention = Attention(b, s)
            attention.run()
        ended = [(c, c.value) for c in b.counters.values()]
        for q in (b.pe, b.act, b.dve, b.pool, b.sp):
            q.wait(*ended)
        with ExitStack() as s:
            FeedForward(b, s).run()
            with nc.Block() as block:
                block.sync(b.sp.replay)
                block.tensor(b.pe.replay)
                block.scalar(b.act.replay)
                block.vector(b.dve.replay)
                block.gpsimd(b.pool.replay)


def kernel(**inputs):
    import concourse.bacc as bacc
    from concourse.bass_utils import run_bass_kernel_spmd

    a = {k: np.asarray(v) for k, v in inputs.items()}
    x, ctxs = a["x"], a["ctx_1024"]
    flat = x.reshape(TOKENS, DIM)

    def rows_by_byte(w):
        return w.reshape(JT, P, 2, 2, P).transpose(4, 0, 3, 2, 1).reshape(P, JT, 4 * P)

    def scales_by_block(w):
        return w.reshape(JT, P, 2, 2, 8).transpose(4, 0, 3, 2, 1).reshape(8, JT, 4 * P)

    arrays = {
        "x": x, "xT": flat.reshape(TOKENS, DC, P).transpose(2, 1, 0),
        "ctx": ctxs, "ctxT": ctxs.reshape(BATCH, SKV, CC, P).transpose(0, 3, 2, 1),
        "Wq": a["L0_xattn_Wq"], "Wk": a["L0_xattn_Wk"], "Wv": a["L0_xattn_Wv"], "Wo": a["L0_xattn_Wo"],
        "gq": a["L0_xattn_gq"].reshape(HD, 1), "gk": a["L0_xattn_gk"].reshape(HD, 1),
        "gate_packed": rows_by_byte(a["L0_ffn_gate_W_packed"]), "gate_scales": scales_by_block(a["L0_ffn_gate_scales"]),
        "up_packed": rows_by_byte(a["L0_ffn_up_W_packed"]), "up_scales": scales_by_block(a["L0_ffn_up_scales"]),
        "down_packed": a["L0_ffn_down_W_packed"].reshape(DIM, JT, P).transpose(2, 1, 0),
        "down_scales": a["L0_ffn_down_scales"].reshape(DIM, JT, 8).transpose(2, 1, 0),
    }
    arrays = {k: np.ascontiguousarray(v) for k, v in arrays.items()}
    nc = bacc.Bacc("TRN2", target_bir_lowering=False, num_devices=1)
    d = {k: nc.dram_tensor(f"in_{k}", v.shape, mybir.dt.from_np(v.dtype), kind="ExternalInput").ap()
         for k, v in arrays.items()}
    d["out"] = nc.dram_tensor("out_yT", (P, DC, TOKENS), F32, kind="ExternalOutput").ap()
    d["x1T"] = nc.dram_tensor("spill_x1T", (P, DC, TOKENS), F32, kind="Internal").ap()
    d["x2T"] = nc.dram_tensor("spill_x2T", (P, DC, TOKENS), F32, kind="Internal").ap()
    build(nc, d)
    r = run_bass_kernel_spmd(nc, [{f"in_{k}": v for k, v in arrays.items()}], core_ids=[0])
    out = r.results[0]["out_yT"]
    return out.transpose(2, 1, 0).reshape(BATCH, SQ, DIM)
```

```python
from contextlib import ExitStack

import numpy as np

import concourse.bass as bass
import concourse.mybir as mybir

F32 = mybir.dt.float32
F32R = mybir.dt.float32r
BF16 = mybir.dt.bfloat16
I32 = mybir.dt.int32
I16 = mybir.dt.int16
ALU = mybir.AluOpType
ACT = mybir.ActivationFunctionType
AX_X = mybir.AxisListType.X

P = 128
BATCH, SQ, DIM = 16, 100, 512
SKV, CDIM = 361, 256
HEADS, HD = 16, 128
MLP = 4096
FP4_BLOCK = 32
EPS = 1e-5
TOKENS = BATCH * SQ
BANK = 512
NBANKS = 8

GB = 4
NG = BATCH // GB
GT = GB * SQ
QH = 4
NQUAD = HEADS // QH
DC = DIM // P
CC = CDIM // P
KT = 3
KP = 122
KPAD = KT * KP
SCOLS = SKV + SKV % 2
LASTK = SKV - (KT - 1) * KP
UNITS = NG * NQUAD * GB

JT = MLP // (2 * P)
NCHUNK = 4
CT = TOKENS // NCHUNK
GELU_C = 0.7978845608028654
GELU_A = 0.044715


class Counter:

    def __init__(self, sem):
        self.sem, self.value = sem, 0

    def after(self, step):
        self.value += step
        return (self, self.value)

    def mark(self):
        return (self, self.value)


class Queue:

    def __init__(self):
        self.steps, self.seen = [], {}

    def wait(self, *marks):
        for counter, value in marks:
            if self.seen.get(counter, 0) < value:
                self.seen[counter] = value
                self.steps.append(lambda e, s=counter.sem, v=value: e.wait_ge(s, v))

    def do(self, emit, counter=None, step=1):
        if counter is None:
            self.steps.append(emit)
            return None
        self.steps.append(lambda e: emit(e).then_inc(counter.sem, step))
        return counter.after(step)

    def replay(self, engine):
        for s in self.steps:
            s(engine)


class Place:

    def __init__(self, t):
        self.t, self.last_use = t, []


class Turns:

    def __init__(self, tensors):
        self.places, self.n = [Place(t) for t in tensors], 0

    def next(self):
        self.n += 1
        return self.places[(self.n - 1) % len(self.places)]


class Builder:
    def __init__(self, nc, ctx, d):
        self.nc, self.ctx, self.d = nc, ctx, d
        self.pe, self.act, self.dve, self.pool, self.sp = (Queue() for _ in range(5))
        self.all_banks = [ctx.enter_context(nc.psum_tensor(f"bank{i}", [P, BANK], F32)) for i in range(NBANKS)]
        self.slow_banks, self.banks = Turns(self.all_banks[:KT]), Turns(self.all_banks[KT:])
        self.counters = {}

    def count(self, name):
        if name not in self.counters:
            self.counters[name] = Counter(self.ctx.enter_context(self.nc.semaphore(name)))
        return self.counters[name]

    def sb(self, stack, name, shape, dt=F32):
        return stack.enter_context(self.nc.sbuf_tensor(name, shape, dt))

    def all_marks(self):
        return [(c, c.value) for c in self.counters.values()]

    def matmul3(self, out, terms, counter):
        passes = [ab for lh, ll, rh, rl in terms for ab in ((lh, rh), (lh, rl), (ll, rh))]
        for i, (a, b) in enumerate(passes):
            first, last = i == 0, i == len(passes) - 1
            mark = self.pe.do(lambda e, a=a, b=b, f=first, l=last: e.matmul(out, a, b, start=f, stop=l),
                              counter if last else None)
        return mark

    def split(self, hi, lo, src, hi_engine, lo_engine, name, ready):
        hi_engine.wait(*ready)
        if hi_engine is self.act:
            m_hi = hi_engine.do(lambda e: e.copy(hi, src), self.count(name + "_hi"))
        else:
            m_hi = hi_engine.do(lambda e: e.tensor_scalar(hi, src, 1.0, 1.0, ALU.mult, ALU.mult),
                                self.count(name + "_hi"))
        lo_engine.wait(*ready, m_hi)
        m_lo = lo_engine.do(lambda e: e.tensor_tensor(lo, src, hi.bitcast(F32), ALU.subtract),
                            self.count(name + "_lo"))
        return [m_hi, m_lo]

    def load(self, dst, src, name, queue=None):
        return (queue or self.sp).do(lambda e: e.dma_start(dst, src), self.count(name), 16)


def build_constants(b, s):
    nc, d = b.nc, b.d
    b.ident = b.sb(s, "ident", [P, P])
    b.power = b.sb(s, "power", [P, QH * GB])
    b.selector_f = b.sb(s, "selector_f", [P, P])
    b.selector = b.sb(s, "selector", [P, QH, P], F32R)
    m = b.pool.do(lambda e: e.memset(b.ident[:, :], 0.0), b.count("s_const"))
    b.pool.wait(m)
    b.const = [b.pool.do(lambda e: e.affine_select(out=b.ident[:, :], in_=b.ident[:, :], compare_op=ALU.not_equal,
                                                   fill=1.0, base=0, pattern=[[-1, P]], channel_multiplier=1),
                         b.count("s_const"))]
    b.const.append(b.pool.do(lambda e: e.memset(b.power[:, :], -0.5), b.count("s_const")))
    m = b.pool.do(lambda e: e.memset(b.selector_f[:, :], 0.0), b.count("s_const"))
    for h in range(QH):
        b.pool.wait(m)
        b.pool.do(lambda e, h=h: e.memset(b.selector_f[:, h:h + 1], 1.0), b.count("s_const"))
        b.pool.wait(b.count("s_const").mark())
        m = b.pool.do(lambda e, h=h: e.tensor_copy(b.selector[:, h, :], b.selector_f[:, :]), b.count("s_const"))
        b.pool.wait(m)
        m = b.pool.do(lambda e, h=h: e.memset(b.selector_f[:, h:h + 1], 0.0), b.count("s_const"))
    b.const.append(m)


class Attention:
    def __init__(self, b, s, lasting):
        self.b = b
        sb = lambda name, shape, dt=F32: b.sb(s, name, shape, dt)
        pair = lambda name, shape: (sb(name + "_hi", shape, F32R), sb(name + "_lo", shape, F32R))
        sl = lambda name, shape: b.sb(lasting, name, shape)
        self.gqk = sl("gqk", [P, 3])
        self.x_raw = Place(sl("x_raw", [SQ, DIM]))
        self.x_norm = Turns([sl(f"x_norm{i}", [SQ, DIM]) for i in range(2)])
        self.ln_small = Turns([sl(f"ln_small{i}", [SQ, 12]) for i in range(2)])
        self.x1T = Place(sl("x1T", [P, DC, GT]))
        self.x1T_done = []
        self.x2T = Place(sl("x2T", [P, DC * SQ]))
        self.x2_spilled = [[] for _ in range(NG)]
        self.x1_spilled = [[] for _ in range(NG)]
        self.ctxT = [pair(f"ctxT{i}", [P, CC, KPAD]) for i in range(GB)]
        self.ctxN = [pair(f"ctxN{i}", [KP, KT, CDIM]) for i in range(GB)]
        self.ctx_ready, self.ctx_used = [[] for _ in range(GB)], [[] for _ in range(GB)]
        self.ctxT_raw = Place(sb("ctxT_raw", [P, CC, KPAD]))
        self.ctxN_raw = Place(sb("ctxN_raw", [KP, KT, CDIM]))
        self.xlnT = pair("xlnT", [P, DC, GT])
        self.xlnT_used, self.xlnT_ready = [], []
        self.qT = [pair(f"qT{h}", [P, GT]) for h in range(QH)]
        self.qT_used, self.qT_ready = [[] for _ in range(QH)], [[] for _ in range(QH)]
        self.queries_tail, self.q_var_ready = None, None
        self.q_sq = Place(sb("q_sq", [P, GT]))
        self.q_sq_split = Turns([pair(f"q_sq{i}", [P, GT]) for i in range(2)])
        self.q_var = Place(sb("q_var", [QH, GT]))
        self.q_rstd = Turns([sb(f"q_rstd{i}", [SQ, GB * QH]) for i in range(2)])
        self.wk, self.wk_raw = pair("wk", [P, CC, QH * HD]), Place(sb("wk_raw", [P, CC, QH * HD]))
        self.wk_used = []
        self.k_sq = Turns([sb(f"k_sq{i}", [KP, QH * HD]) for i in range(1)])
        self.k_ss = Turns([sb(f"k_ss{i}", [KP, KT * QH]) for i in range(2)])
        self.khat = Place(sb("khat", [KP, KT, QH * HD]))
        self.kT = pair("kT", [P, QH, KPAD])
        self.kT_used, self.kT_ready = [], []
        self.attn = [Place(sb(f"attn{h}", [SQ, KPAD])) for h in range(QH)]
        self.stats = Turns([sb(f"stats{i}", [SQ, 3 * QH]) for i in range(2)])
        self.aT = pair("aT", [KP, KT, QH * SQ])
        self.aT_used, self.aT_ready = [], []
        self.yT = pair("yT", [P, CC, QH, GT])
        self.yT_used, self.yT_ready = [], []
        self.oT = Turns([pair(f"oT{i}", [P, GT]) for i in range(2)])
        self.head_w = Turns([pair(f"head_w{i}", [P, DIM]) for i in range(3)])
        self.head_raw = Turns([sb(f"head_raw{i}", [P, DIM]) for i in range(2)])
        self.wv_ring = Turns([pair(f"wv{i}", [P, CC * HD]) for i in range(2)])
        self.wv_raw = Turns([sb(f"wv_raw{i}", [P, CC * HD]) for i in range(2)])
        self.head_queue, self.wv_queue = [], []

    def setup(self):
        b = self.b
        m = [b.load(self.gqk[:, 0:1], b.d["gq"], "d_gq"), b.load(self.gqk[:, 1:2], b.d["gk"], "d_gk")]
        b.dve.wait(*m)
        self.gqk_ready = b.dve.do(lambda e: e.scalar_tensor_tensor(
            out=self.gqk[:, 2:3], in0=self.gqk[:, 0:1], scalar=float(HD) ** -0.5, in1=self.gqk[:, 1:2],
            op0=ALU.mult, op1=ALU.mult), b.count("s_gqk"))
        self.pads = [b.dve.do(lambda e: e.memset(self.ctxT_raw.t[:, :, SKV:KPAD], 0.0), b.count("s_pad")),
                     b.dve.do(lambda e: e.memset(self.ctxN_raw.t[96:KP, KT - 1, :], 0.0), b.count("s_pad"))]
        for h in range(QH):
            self.pads.append(b.dve.do(lambda e, h=h: e.memset(self.attn[h].t[:, SKV:KPAD], 0.0), b.count("s_pad")))

    def load_ctx(self, batch, hi_engine=None, lo_engine=None):
        b, i = self.b, batch % GB
        b.sp.wait(*self.pads, *self.ctxT_raw.last_use, *self.ctxN_raw.last_use)
        mT = b.load(self.ctxT_raw.t[:, :, 0:SKV], b.d["ctxT"][batch], "d_ctxT")
        mN = [b.load(self.ctxN_raw.t[:, 0:KT - 1, :],
                     b.d["ctx"][batch, 0:(KT - 1) * KP, :].rearrange("(t p) c -> p t c", p=KP), "d_ctxN"),
              b.load(self.ctxN_raw.t[0:LASTK, KT - 1, :], b.d["ctx"][batch, (KT - 1) * KP:SKV, :], "d_ctxN2")]
        tag = "_first" if hi_engine else ""
        hi_engine, lo_engine = hi_engine or b.pool, lo_engine or b.pool
        for q in {hi_engine, lo_engine}:
            q.wait(*self.ctx_used[i])
        (th, tl), (nh, nl) = self.ctxT[i], self.ctxN[i]
        mT = b.split(th[:, :, :], tl[:, :, :], self.ctxT_raw.t[:, :, :], hi_engine, lo_engine, "s_ctxT" + tag, [mT])
        mN = b.split(nh[:, :, :], nl[:, :, :], self.ctxN_raw.t[:, :, :], hi_engine, lo_engine, "s_ctxN" + tag, mN)
        self.ctxT_raw.last_use, self.ctxN_raw.last_use = mT, mN
        self.ctx_ready[i], self.ctx_used[i] = mT + mN, []

    def load_wk(self, quad, hi_engine=None, lo_engine=None):
        b = self.b
        b.sp.wait(*self.wk_raw.last_use)
        src = b.d["Wk"][:, quad * QH * HD:(quad + 1) * QH * HD].rearrange("(c p) n -> p c n", p=P)
        m = b.load(self.wk_raw.t[:, :, :], src, "d_wk")
        tag = "_first" if hi_engine else ""
        hi_engine, lo_engine = hi_engine or b.pool, lo_engine or b.pool
        for q in {hi_engine, lo_engine}:
            q.wait(*self.wk_used)
        self.wk_used = []
        self.wk_ready = b.split(self.wk[0][:, :, :], self.wk[1][:, :, :], self.wk_raw.t[:, :, :],
                                hi_engine, lo_engine, "s_wk" + tag, [m])
        self.wk_raw.last_use = self.wk_ready

    def load_head_weight(self, kind, head):
        b = self.b
        raw = self.head_raw.next()
        b.sp.wait(*raw.last_use)
        if kind == "q":
            src = b.d["Wq"][:, head * HD:(head + 1) * HD].rearrange("(c p) n -> p c n", p=P)
            dst = raw.t[:, :].rearrange("p (c n) -> p c n", c=DC)
        else:
            src, dst = b.d["Wo"][head * HD:(head + 1) * HD, :], raw.t[:, :]
        m = b.load(dst, src, f"d_head{self.head_raw.n % 2}")
        slot = self.head_w.next()
        b.pool.wait(*slot.last_use)
        raw.last_use = b.split(slot.t[0][:, :], slot.t[1][:, :], raw.t[:, :], b.pool, b.pool, "s_headw", [m])
        self.head_queue.append((slot, raw.last_use))

    def load_wv(self, head):
        b = self.b
        raw = self.wv_raw.next()
        b.sp.wait(*raw.last_use)
        src = b.d["Wv"][:, head * HD:(head + 1) * HD].rearrange("(c p) n -> p c n", p=P)
        m = b.load(raw.t[:, :].rearrange("p (c n) -> p c n", c=CC), src, f"d_wv{self.wv_raw.n % 2}")
        slot = self.wv_ring.next()
        b.pool.wait(*slot.last_use)
        raw.last_use = b.split(slot.t[0][:, :], slot.t[1][:, :], raw.t[:, :], b.pool, b.pool, "s_wv", [m])
        self.wv_queue.append((slot, raw.last_use))

    def moments(self, src, ready):
        b = self.b
        small = self.ln_small.next()
        st = small.t
        b.dve.wait(*small.last_use, *ready)
        m = b.dve.do(lambda e: e.bn_stats(st[:, 0:6], src), b.count("s_bn"))
        b.dve.wait(m)
        m = b.dve.do(lambda e: e.bn_aggr(st[:, 6:8], st[:, 0:6]), b.count("s_bn"))
        b.dve.wait(m)
        m = b.dve.do(lambda e: e.tensor_scalar(st[:, 8:9], st[:, 7:8], EPS, None, ALU.add), b.count("s_bn"))
        b.pool.wait(m, *b.const)
        m = b.pool.do(lambda e: e.tensor_tensor(st[:, 9:10], st[:, 8:9], b.power[0:SQ, 0:1], ALU.pow),
                      b.count("s_lnrstd"))
        return small, m

    def normalise(self, src, moments):
        b = self.b
        small, m = moments
        st, norm = small.t, self.x_norm.next()
        b.dve.wait(m, *norm.last_use)
        m = b.dve.do(lambda e: e.tensor_scalar(norm.t[:, :], src, st[:, 6:7], st[:, 9:10], ALU.subtract, ALU.mult),
                     b.count("s_xnorm"))
        small.last_use = [m]
        return norm, m

    def norm_transposed(self, norm, ready, parity):
        b = self.b
        bank = b.banks.next()
        b.pe.wait(*bank.last_use)
        b.pe.wait(ready, *b.const)
        for c in range(DC):
            if parity:
                lo = (c // 2) * 2 * P + c % 2
                src = norm.t[:, lo:lo + 2 * P - 1:2]
            else:
                src = norm.t[:, c * P:(c + 1) * P]
            m = b.pe.do(lambda e, c=c, src=src: e.transpose(bank.t[:, c * SQ:(c + 1) * SQ], src, b.ident[0:SQ, 0:SQ]),
                        b.count("s_normT") if c == DC - 1 else None)
        norm.last_use = [m]
        return bank, m

    def load_tokens(self, batch):
        self.b.sp.wait(*self.x_raw.last_use)
        self.x_loaded = self.b.load(self.x_raw.t[:, :], self.b.d["x"][batch], "d_x")

    def ln1(self, batch):
        b, i, kept = self.b, batch % GB, {}

        def first():
            kept["moments"] = self.moments(self.x_raw.t[:, :], [self.x_loaded])

        def second():
            kept["norm"] = self.normalise(self.x_raw.t[:, :], kept["moments"])
            self.x_raw.last_use = [kept["norm"][1]]

        def third():
            bank, m = self.norm_transposed(*kept["norm"], False)
            if i == 0:
                b.act.wait(*self.xlnT_used)
                b.dve.wait(*self.xlnT_used)
                self.xlnT_used, self.xlnT_ready = [], []
            cols = slice(i * SQ, (i + 1) * SQ)
            bank.last_use = b.split(self.xlnT[0][:, :, cols], self.xlnT[1][:, :, cols],
                                    bank.t[:, 0:DC * SQ].rearrange("p (c n) -> p c n", c=DC), b.act, b.dve, "s_xlnT", [m])
            self.xlnT_ready += bank.last_use

        return [first, second, third]

    def queries(self, loads):
        b = self.b
        xh, xl = self.xlnT
        sbank = b.banks.next()
        b.pe.wait(*sbank.last_use)
        ssum = sbank.t[:, 0:GT]
        squares = []

        def add_squares(h):
            place, ready = squares[h]
            b.pe.wait(*ready, *b.const)
            for k in range(2):
                m = b.pe.do(lambda e, k=k: e.matmul(ssum, b.selector[:, h, :], place.t[k][:, :],
                                                    start=h == 0 and k == 0, stop=h == QH - 1 and k == 1),
                            b.count("s_qss") if k else None)
            place.last_use = [m]
            return m

        for h in range(QH):
            slot, wready = self.head_queue.pop(0)
            wh, wl = slot.t
            bank = b.slow_banks.next()
            b.pe.wait(*bank.last_use)
            b.pe.wait(*wready, *self.xlnT_ready)
            q = bank.t[:, 0:GT]
            m = b.matmul3(q, [(wh[:, c * HD:(c + 1) * HD], wl[:, c * HD:(c + 1) * HD], xh[:, c, :], xl[:, c, :])
                              for c in range(DC)], b.count("s_q"))
            slot.last_use = self.xlnT_used = [m]
            b.act.wait(m, *self.q_sq.last_use)
            m2 = b.act.do(lambda e, q=q: e.activation(self.q_sq.t[:, :], q, ACT.Square), b.count("s_qsq"))
            place = self.q_sq_split.next()
            b.act.wait(*place.last_use)
            b.dve.wait(*place.last_use)
            sh, sl = place.t
            ready = self.q_sq.last_use = b.split(sh[:, :], sl[:, :], self.q_sq.t[:, :], b.act, b.dve, "s_qsqs", [m2])
            b.act.wait(*self.qT_used[h], self.gqk_ready)
            b.dve.wait(*self.qT_used[h])
            qh, ql = self.qT[h]
            m3 = b.act.do(lambda e, q=q, o=qh: e.activation(o[:, :], q, ACT.Copy, scale=self.gqk[:, 2:3]), b.count("s_qT_hi"))
            b.dve.wait(m3)
            m4 = b.dve.do(lambda e, q=q, o=ql, hi=qh: e.scalar_tensor_tensor(
                out=o[:, :], in0=q, scalar=self.gqk[:, 2:3], in1=hi[:, :].bitcast(F32), op0=ALU.mult, op1=ALU.subtract),
                b.count("s_qT_lo"))
            bank.last_use = [m2, m4]
            self.qT_ready[h], self.qT_used[h] = [m3, m4], []
            squares.append((place, ready))
            if h > 0:
                add_squares(h - 1)
            self.load_head_weight(*loads[h])
        self.queries_tail = (add_squares, sbank, ssum)

    def queries_squares(self):
        if self.queries_tail is None:
            return
        b = self.b
        add_squares, sbank, ssum = self.queries_tail
        self.queries_tail = None
        m = add_squares(QH - 1)
        b.dve.wait(m, *self.q_var.last_use)
        m = b.dve.do(lambda e: e.tensor_scalar(self.q_var.t[:, :], ssum[0:QH, :], 1.0 / HD, EPS, ALU.mult, ALU.add),
                     b.count("s_qvar"))
        sbank.last_use = [m]
        self.q_var_ready = m

    def queries_rstd(self):
        if self.q_var_ready is None:
            return
        b, m = self.b, self.q_var_ready
        self.q_var_ready = None
        bank = b.banks.next()
        b.pe.wait(*bank.last_use)
        b.pe.wait(m)
        for i in range(GB):
            m = b.pe.do(lambda e, i=i: e.transpose(bank.t[0:SQ, i * QH:(i + 1) * QH], self.q_var.t[:, i * SQ:(i + 1) * SQ],
                                                   b.ident[0:QH, 0:QH]), b.count("s_qvarT") if i == GB - 1 else None)
        self.q_var.last_use = [m]
        rstd = self.q_rstd.next()
        b.dve.wait(m, *rstd.last_use)
        m = b.dve.do(lambda e: e.tensor_copy(rstd.t[:, :], bank.t[0:SQ, 0:GB * QH]), b.count("s_qvarT_sb"))
        bank.last_use = [m]
        b.pool.wait(m, *b.const)
        m = b.pool.do(lambda e: e.tensor_tensor(rstd.t[:, :], rstd.t[:, :], b.power[0:SQ, 0:GB * QH], ALU.pow),
                      b.count("s_qrstd"))
        self.rstd_q, self.rstd_q_ready = rstd, m

    def keys(self, unit, tiles):
        b, i = self.b, unit % GB
        if 0 in tiles:
            self.k_tiles, self.khat_ready = [], []
            self.k_rstd = self.k_ss.next()
        ss = self.k_rstd
        th, tl = self.ctxT[i]
        wh, wl = self.wk
        b.pe.wait(*self.ctx_ready[i], *self.wk_ready)
        for t in tiles:
            bank = b.slow_banks.next()
            b.pe.wait(*bank.last_use)
            ks = slice(t * KP, (t + 1) * KP)
            m = b.matmul3(bank.t[0:KP, :], [(th[:, c, ks], tl[:, c, ks], wh[:, c, :], wl[:, c, :]) for c in range(CC)],
                          b.count("s_k"))
            self.wk_used = self.ctx_used[i] = [m]
            sq, cols = self.k_sq.next(), ss.t[:, t * QH:(t + 1) * QH]
            b.act.wait(m, *sq.last_use)
            m = b.act.do(lambda e, s=sq, k=bank: e.activation(s.t[:, :], k.t[0:KP, :], ACT.Square), b.count("s_ksq"))
            b.dve.wait(m, *ss.last_use)
            m = b.dve.do(lambda e, s=sq, o=cols: e.tensor_reduce(
                o, s.t[:, :].rearrange("p (h d) -> p h d", h=QH), AX_X, ALU.add), b.count("s_kss"))
            sq.last_use = [m]
            b.pool.wait(m, *b.const)
            m = b.pool.do(lambda e, o=cols: e.tensor_scalar(o, o, 1.0 / HD, EPS, ALU.mult, ALU.add), b.count("s_kvar"))
            b.pool.wait(m)
            m = b.pool.do(lambda e, o=cols: e.tensor_tensor(o, o, b.power[0:KP, 0:QH], ALU.pow), b.count("s_krstd"))
            self.k_tiles.append((bank, m))

    def normalise_keys(self, tiles):
        b, ss = self.b, self.k_rstd
        for t in tiles:
            bank, m = self.k_tiles[t]
            b.dve.wait(m, *self.khat.last_use)
            m = b.dve.do(lambda e, t=t, k=bank: e.tensor_tensor(
                self.khat.t[:, t, :].rearrange("p (h d) -> p h d", h=QH),
                k.t[0:KP, :].rearrange("p (h d) -> p h d", h=QH),
                ss.t[:, t * QH:(t + 1) * QH].unsqueeze(2).broadcast_to([KP, QH, HD]), ALU.mult), b.count("s_khat"))
            bank.last_use = [m]
            self.khat_ready.append(m)
            ss.last_use = [m]

    def transpose_keys(self):
        b = self.b
        b.pe.wait(*b.const)
        b.act.wait(*self.kT_used)
        b.dve.wait(*self.kT_used)
        self.kT_ready = []
        kh, kl = self.kT
        for t in range(KT):
            bank = b.banks.next()
            b.pe.wait(self.khat_ready[t], *bank.last_use)
            for h in range(QH):
                m = b.pe.do(lambda e, t=t, h=h, k=bank: e.transpose(
                    k.t[:, h * KP:(h + 1) * KP], self.khat.t[:, t, h * HD:(h + 1) * HD], b.ident[0:KP, 0:KP]),
                    b.count("s_kTp") if h == QH - 1 else None)
            ks = slice(t * KP, (t + 1) * KP)
            bank.last_use = b.split(kh[:, :, ks], kl[:, :, ks], bank.t[:, 0:QH * KP].rearrange("p (h n) -> p h n", h=QH),
                                   b.act, b.dve, "s_kT", [m])
            self.kT_ready += bank.last_use
        self.khat.last_use = [m]

    def scores(self, unit, before_sums, between):
        b, i = self.b, unit % GB
        st = self.stats.next()
        b.dve.wait(*st.last_use)
        neg, total, inv = (st.t[:, k * QH:(k + 1) * QH] for k in range(3))
        rq = self.rstd_q.t
        b.act.wait(*self.pads)
        maxima, exps, self.attn_ready = [], [], []

        def exponentials(h):
            bank, m = maxima[h]
            col = slice(i * QH + h, i * QH + h + 1)
            b.dve.wait(m, self.rstd_q_ready)
            m = b.dve.do(lambda e: e.tensor_tensor(neg[:, h:h + 1], neg[:, h:h + 1], rq[:, col], ALU.mult),
                         b.count("s_negmax"))
            b.act.wait(m, *self.attn[h].last_use)
            exps.append(b.act.do(lambda e: e.activation(
                self.attn[h].t[:, 0:SKV], bank.t[0:SQ, 0:SKV], ACT.Exp, bias=neg[:, h:h + 1], scale=rq[:, col],
                accum_out=total[:, h:h + 1]), b.count("s_exp")))
            bank.last_use = [exps[h]]

        def inverse(first, last):
            b.dve.wait(exps[last])
            return b.dve.do(lambda e: e.reciprocal(inv[:, first:last + 1], total[:, first:last + 1]), b.count("s_inv"))

        for h in range(QH):
            bank = b.banks.next()
            b.pe.wait(*bank.last_use)
            qs = slice(i * SQ, (i + 1) * SQ)
            (qh, ql), (kh, kl) = self.qT[h], self.kT
            b.pe.wait(*self.kT_ready, *self.qT_ready[h])
            m = b.matmul3(bank.t[0:SQ, 0:SCOLS], [(qh[:, qs], ql[:, qs], kh[:, h, 0:SCOLS], kl[:, h, 0:SCOLS])],
                          b.count("s_sc"))
            self.kT_used, self.qT_used[h] = [m], [m]
            b.dve.wait(m)
            m2 = b.dve.do(lambda e, h=h, k=bank: e.tensor_reduce(neg[:, h:h + 1], k.t[0:SQ, 0:SKV], AX_X, ALU.max,
                                                                 negate=True), b.count("s_max"))
            maxima.append((bank, m2))
            if h > 0:
                exponentials(h - 1)
        exponentials(QH - 1)
        before_sums()
        inverses = [inverse(h, h) for h in range(QH // 2)]
        for h, m in enumerate(inverses):
            b.dve.wait(m)
            self.attn_ready.append(b.dve.do(lambda e, h=h: e.tensor_scalar(
                self.attn[h].t[:, 0:SKV], self.attn[h].t[:, 0:SKV], inv[:, h:h + 1], None, ALU.mult), b.count("s_attn")))
        between()
        self.inverse_rest = inverse(QH // 2, QH - 1)
        self.rstd_q.last_use = exps
        self.stats_now = st

    def normalise_rest(self):
        b, st = self.b, self.stats_now
        b.act.wait(self.inverse_rest)
        for h in range(QH // 2, QH):
            self.attn_ready.append(b.act.do(lambda e, h=h: e.activation(
                self.attn[h].t[:, 0:SKV], self.attn[h].t[:, 0:SKV], ACT.Copy, scale=st.t[:, 2 * QH + h:2 * QH + h + 1]),
                b.count("s_attn_rest")))
        st.last_use = [self.attn_ready[QH // 2 - 1], self.attn_ready[-1]]

    def transpose_attn(self, between):
        b = self.b
        ah, al = self.aT
        b.act.wait(*self.aT_used)
        b.dve.wait(*self.aT_used)
        self.aT_used, self.aT_ready = [], []
        banks = [b.banks.next() for _ in range(KT)]
        for bank in banks:
            b.pe.wait(*bank.last_use)
        for h in range(QH):
            b.pe.wait(self.attn_ready[h])
            for t, bank in enumerate(banks):
                m = b.pe.do(lambda e, t=t, h=h, k=bank: e.transpose(
                    k.t[0:KP, h * SQ:(h + 1) * SQ], self.attn[h].t[:, t * KP:(t + 1) * KP], b.ident[0:SQ, 0:SQ]),
                    b.count("s_aTp"))
            self.attn[h].last_use = [m]
        between()
        for t, bank in enumerate(banks):
            bank.last_use = b.split(ah[:, t, :], al[:, t, :], bank.t[0:KP, 0:QH * SQ], b.act, b.dve, "s_aT", [m])
            self.aT_ready += bank.last_use

    def attend(self, unit):
        b, i = self.b, unit % GB
        (ah, al), (nh, nl), (yh, yl) = self.aT, self.ctxN[i], self.yT
        b.pe.wait(*self.aT_ready)
        if i == 0:
            b.act.wait(*self.yT_used)
            b.dve.wait(*self.yT_used)
            self.yT_used, self.yT_ready = [], []
        for c in range(CC):
            bank = b.banks.next()
            b.pe.wait(*bank.last_use)
            cs = slice(c * P, (c + 1) * P)
            m = b.matmul3(bank.t[:, 0:QH * SQ], [(nh[:, t, cs], nl[:, t, cs], ah[:, t, :], al[:, t, :]) for t in range(KT)],
                          b.count("s_y"))
            qs = slice(i * SQ, (i + 1) * SQ)
            bank.last_use = b.split(yh[:, c, :, qs], yl[:, c, :, qs],
                                   bank.t[:, 0:QH * SQ].rearrange("p (h n) -> p h n", h=QH), b.act, b.dve, "s_yT", [m])
            self.yT_ready += bank.last_use
        self.aT_used = [m]
        self.ctx_used[i] = self.ctx_used[i] + [m]

    def project(self, group, quad, weights, beside):
        b = self.b
        if quad == 0:
            b.sp.wait(*self.x1T.last_use)
            m = b.load(self.x1T.t[:, :, :], b.d["xT"][:, :, group * GT:(group + 1) * GT], "d_xT")
            self.x1T_done = [m]
        yh, yl = self.yT
        heads = []

        def value(h):
            slot, wready = self.wv_queue.pop(0)
            wh, wl = slot.t
            bank = b.slow_banks.next()
            b.pe.wait(*bank.last_use)
            b.pe.wait(*wready, *self.yT_ready)
            m = b.matmul3(bank.t[:, 0:GT], [(wh[:, c * HD:(c + 1) * HD], wl[:, c * HD:(c + 1) * HD],
                                             yh[:, c, h, :], yl[:, c, h, :]) for c in range(CC)], b.count("s_o"))
            slot.last_use = [m]
            self.yT_used = [m]
            o = self.oT.next()
            b.act.wait(*o.last_use)
            b.dve.wait(*o.last_use)
            bank.last_use = b.split(o.t[0][:, :], o.t[1][:, :], bank.t[:, 0:GT], b.act, b.dve, "s_oT", [m])
            heads.append((o, bank.last_use))
            if h + 2 < QH:
                self.load_wv(quad * QH + h + 2)

        value(0)
        value(1)
        beside()
        outs = [b.banks.next() for _ in range(DC)]
        for bank in outs:
            b.pe.wait(*bank.last_use)
        for h in range(QH):
            slot, wready = self.head_queue.pop(0)
            wh, wl = slot.t
            o, oready = heads[h]
            b.pe.wait(*wready, *oready)
            for c in range(DC):
                cs = slice(c * P, (c + 1) * P)
                out = outs[c].t[:, 0:GT]
                for k, (a, r) in enumerate(((wh, o.t[0]), (wh, o.t[1]), (wl, o.t[0]))):
                    f, l = h == 0 and k == 0, h == QH - 1 and k == 2
                    m = b.pe.do(lambda e, out=out, a=a, r=r, cs=cs, f=f, l=l: e.matmul(
                        out, a[:, cs], r[:, :], start=f, stop=l),
                        b.count("s_out") if k == 2 and (c == DC - 1 or h == QH - 1) else None)
                if h == QH - 1:
                    b.dve.wait(m, *self.x1T_done)
                    md = b.dve.do(lambda e, c=c, out=out: e.tensor_tensor(self.x1T.t[:, c, :], out, self.x1T.t[:, c, :],
                                                                          ALU.add), b.count("s_x1T"))
                    outs[c].last_use = [md]
            slot.last_use = [m]
            o.last_use = [m]
            if h + 2 < QH:
                value(h + 2)
            beside()
            if weights:
                self.load_head_weight(*weights.pop(0))
        self.x1T_done = [md]

    def spill_x1(self, group):
        b = self.b
        b.sp.wait(*self.x1T_done)
        self.x1_spilled[group] = [b.sp.do(
            lambda e: e.dma_start(b.d["x1T"][:, :, group * GT:(group + 1) * GT], self.x1T.t[:, :, :]), b.count("d_x1T_out"), 16)]
        self.x1T.last_use = list(self.x1_spilled[group])

    def ln2(self, group, j):
        b, kept = self.b, {}

        def first():
            bank = b.banks.next()
            b.pe.wait(*bank.last_use)
            b.pe.wait(*self.x1T_done)
            for c in range(DC):
                m = b.pe.do(lambda e, c=c: e.transpose(
                    bank.t[0:SQ, c * P:(c + 1) * P], self.x1T.t[:, c, j * SQ:(j + 1) * SQ], b.ident[:, :]),
                    b.count("s_x1") if c == DC - 1 else None)
            self.x1T.last_use = self.x1T.last_use + [m]
            kept["bank"], kept["moments"] = bank, self.moments(bank.t[0:SQ, :], [m])
            bank.last_use = None

        def second():
            kept["norm"] = self.normalise(kept["bank"].t[0:SQ, :], kept["moments"])
            kept["bank"].last_use = [kept["norm"][1]]

        def third():
            bank, m = self.norm_transposed(*kept["norm"], True)
            b.act.wait(m, *self.x2T.last_use)
            m = b.act.do(lambda e: e.copy(self.x2T.t[:, :], bank.t[:, 0:DC * SQ]), b.count("s_x2T"))
            bank.last_use = [m]
            b.sp.wait(m)
            cols = slice(group * GT + j * SQ, group * GT + (j + 1) * SQ)
            m = b.sp.do(lambda e: e.dma_start(b.d["x2T"][:, :, cols], self.x2T.t[:, :].rearrange("p (c n) -> p c n", c=DC)),
                        b.count("d_x2T_out"), 16)
            self.x2T.last_use = [m]
            self.x2_spilled[group].append(m)

        return [first, second, third]

    def step(self):
        if self.steps:
            self.steps.pop(0)()

    def run(self, feed_forward):
        b = self.b
        self.steps = []
        self.setup()
        early = (b.act, b.dve)
        norms = [self.ln1(i) for i in range(GB)]
        self.load_tokens(0)
        norms[0][0]()
        self.load_ctx(0, *early)
        norms[0][1]()
        self.load_tokens(1)
        self.load_wk(0, *early)
        norms[1][0]()
        self.keys(0, range(KT))
        norms[0][2]()
        norms[1][1]()
        for i in range(2, GB):
            self.load_tokens(i)
            norms[i][0]()
            norms[i - 1][2]()
            norms[i][1]()
            self.load_head_weight("q", i - 2)
        norms[GB - 1][2]()
        self.load_head_weight("q", 2)
        self.normalise_keys(range(KT))
        self.queries([("q", 3 + h) for h in range(QH)])
        self.queries_squares()
        self.queries_rstd()
        for i in range(1, GB):
            self.load_ctx(i)
        pending, beside = None, lambda: None
        for u in range(UNITS + 1):
            group, quad, i = u // (NQUAD * GB), u // GB % NQUAD, u % GB
            last_quad, qn = quad == NQUAD - 1, u // GB + 1
            if u < UNITS:
                ahead = i + 1 - GB * (NQUAD - 1 - quad)
                if ahead in range(GB) and group + 1 < NG:
                    self.steps += self.ln1((group + 1) * GB + ahead)
                elif quad == 0 and group > 0 and i > 0:
                    for j in (range(i - 1, i) if i < 3 else range(2, GB)):
                        self.steps += self.ln2(group - 1, j)
                self.transpose_keys()
                self.queries_rstd()
                if u + 1 < UNITS:
                    self.keys(u + 1, [0])
                self.step()
                if u + 1 < UNITS:
                    self.keys(u + 1, [1])
                if i == 1:
                    for h in range(2):
                        self.load_wv(quad * QH + h)
                elif last_quad and i == GB - 1 and group + 1 < NG:
                    self.load_ctx((group + 1) * GB + 1)
                elif quad == 0 and group > 0 and i == 0:
                    self.load_ctx(group * GB + 2)
                self.scores(u, self.step, lambda: self.normalise_keys([0] if u + 1 < UNITS else []))
                if u + 1 < UNITS:
                    self.keys(u + 1, [2])
                    self.normalise_keys([1])
                self.normalise_rest()
            if u > 0:
                self.attend(u - 1)
            if u < UNITS:
                if u + 1 < UNITS:
                    self.normalise_keys([2])
                    if i == GB - 1:
                        self.queries([("q", qn % NQUAD * QH + 3)] + [("o", quad * QH + h) for h in range(3)])
                self.step()
                self.transpose_attn(self.queries_squares)
            else:
                self.units_done = b.all_marks()
                beside = feed_forward.begin()
            if i == 2 and qn < NG * NQUAD:
                self.load_wk(qn % NQUAD)
            if ahead + 1 in range(GB) and group + 1 < NG:
                self.load_tokens((group + 1) * GB + ahead + 1)
            if last_quad and i == 1 and group + 1 < NG:
                self.load_ctx((group + 1) * GB)
            elif u < UNITS and quad == 0 and group > 0 and i == 0:
                self.load_ctx(group * GB + 3)
            if pending is not None:
                g, q = pending
                nextq = g * NQUAD + q + 2
                weights = [("o", q * QH + 3)]
                if nextq < NG * NQUAD:
                    weights += [("q", nextq % NQUAD * QH + h) for h in range(3)]
                elif nextq == NG * NQUAD:
                    weights += [("o", (q + 1) * QH + h) for h in range(3)]
                self.project(g, q, weights, beside)
                if q == NQUAD - 1:
                    self.spill_x1(g)
                pending = None
            if u >= UNITS:
                break
            if i == GB - 1:
                pending = (group, quad)
        self.steps = [f for j in range(GB) for f in self.ln2(NG - 1, j)]


class FeedForward:

    def __init__(self, b, s, attention):
        self.b, self.attention = b, attention
        sb = lambda name, shape, dt=F32: b.sb(s, name, shape, dt)
        pair = lambda name, shape: (sb(name + "_hi", shape, F32R), sb(name + "_lo", shape, F32R))
        names = ("gate", "up", "down")
        weights, packed, scale = ([[], [], []] for _ in range(3))

        def weight_places(i):
            for k, n in enumerate(names):
                weights[k].append(pair(f"{n}{i}", [P, 4 * 2 * P]))
                packed[k].append(sb(f"{n}_packed{i}", [P, 4 * P], I32))
                scale[k].append(sb(f"{n}_scale{i}", [P, 4 * P]))

        weight_places(0)
        t16 = lambda name, dt: Place(sb(name, [P, 4 * P], dt))
        self.sign, self.mag = t16("sign", I16), t16("mag", I16)
        self.half, self.over4, self.over6 = t16("half", BF16), t16("over4", BF16), t16("over6", BF16)
        self.value = Turns([sb(f"value{i}", [P, 4 * P], BF16) for i in range(2)])
        self.wide = Turns([sb(f"wide{i}", [P, 4 * P]) for i in range(2)])
        self.xT = pair("xT", [P, DC, TOKENS])
        self.x_raw = Place(sb("xT_raw", [P, DC, CT]))
        self.x_ready = [None] * NCHUNK
        self.sq = Turns([sb(f"sq{i}", [P, CT]) for i in range(2)])
        self.tanh = Turns([sb(f"tanh{i}", [P, CT]) for i in range(2)])
        self.act = Turns([sb(f"act{i}", [P, CT]) for i in range(2)])
        self.inter = Turns([pair(f"inter{i}", [P, CT]) for i in range(4)])
        self.yT = sb("yT", [P, DC, TOKENS])
        self.y_done = [[] for _ in range(NCHUNK)]
        weight_places(1)
        self.weights, self.packed, self.scale = ([Turns(t) for t in x] for x in (weights, packed, scale))

    def load_x(self, ch):
        b, cols = self.b, slice(ch * CT, (ch + 1) * CT)
        raw = self.x_raw
        b.sp.wait(*raw.last_use, *self.attention.x2_spilled[ch])
        m = b.load(raw.t[:, :, :], b.d["x2T"][:, :, cols], "d_x2T")
        raw.last_use = self.x_ready[ch] = b.split(self.xT[0][:, :, cols], self.xT[1][:, :, cols], raw.t[:, :, :],
                                                  b.act, b.dve, "s_xT", [m])

    def load_y(self, ch):
        b, cols = self.b, slice(ch * CT, (ch + 1) * CT)
        b.sp.wait(*self.attention.x1_spilled[ch])
        self.y_done[ch] = [b.load(self.yT[:, :, cols], b.d["x1T"][:, :, cols], f"d_yT{ch}")]

    def fetch(self, jt):
        b, self.fetched = self.b, []
        for k, name in enumerate(("gate", "up", "down")):
            packed, scale = self.packed[k].next(), self.scale[k].next()
            b.sp.wait(*packed.last_use, *scale.last_use)
            m = [b.load(packed.t[:, :], b.d[name + "_packed"][:, jt, :], f"d_{name}{jt % 2}"),
                 b.load(scale.t[:, :], b.d[name + "_scales"][:, jt, :].unsqueeze(1).broadcast_to([8, 16, 4 * P]),
                        f"d_{name}_s{jt % 2}")]
            self.fetched.append((packed, scale, m))

    def decode(self, k, nibble):
        b, kept = self.b, {}
        count = b.count("s_decode")
        dve = lambda emit: b.dve.do(emit, count)
        packed, scale, ready = self.fetched[k]
        codes = packed.t[:, :].bitcast(I16)[:, 0:8 * P:2]
        sign, mag, half, over4, over6 = (x.t[:, :] for x in (self.sign, self.mag, self.half, self.over4, self.over6))

        def bits():
            b.dve.wait(*ready, *self.sign.last_use, *self.mag.last_use)
            dve(lambda e: e.tensor_scalar(sign, codes, 8 << 4 * nibble, 12 - 4 * nibble, ALU.bitwise_and,
                                          ALU.logical_shift_left))
            m = dve(lambda e: e.tensor_scalar(mag, codes, 4 * nibble, 7, ALU.logical_shift_right, ALU.bitwise_and))
            b.act.wait(m, *self.half.last_use)
            self.mag.last_use = kept["half"] = [b.act.do(lambda e: e.activation(half, mag, ACT.Copy, scale=0.5),
                                                         b.count("s_half"))]
            kept["mag"] = m

        def over():
            b.dve.wait(kept["mag"])
            dve(lambda e: e.tensor_scalar(over4, mag, 4.0, 0.5, ALU.max, ALU.mult))
            kept["over"] = dve(lambda e: e.tensor_scalar(over6, mag, 7.0, -2.0, ALU.is_ge, ALU.add))

        def both():
            b.dve.wait(kept["over"])
            kept["both"] = dve(lambda e: e.tensor_tensor(over4, over4, over6, ALU.add))

        def total():
            value = kept["value"] = self.value.next()
            b.dve.wait(kept["both"], *kept["half"], *value.last_use)
            m = dve(lambda e: e.tensor_tensor(value.t[:, :], over4, half, ALU.add))
            self.half.last_use = kept["total"] = [m]

        def signed():
            value = kept["value"]
            v = value.t[:, :].bitcast(I16)
            b.dve.wait(*kept["total"])
            m = dve(lambda e: e.tensor_tensor(v, v, sign, ALU.bitwise_or))
            self.sign.last_use = [m]
            wide = self.wide.next()
            b.pool.wait(m, *ready, *wide.last_use)
            m = b.pool.do(lambda e: e.tensor_tensor(wide.t[:, :], value.t[:, :], scale.t[:, :], ALU.mult),
                          b.count("s_scaled"))
            value.last_use = [m]
            if nibble == 0:
                slot = self.weights[k].next()
                b.act.wait(*slot.last_use)
                b.pool.wait(*slot.last_use)
                self.building[k] = (slot, [])
            slot, marks = self.building[k]
            if k < 2:
                view = lambda t: t[:, :].rearrange("p (r z n) -> p r z n", r=2, z=2)[:, :, nibble, :]
                src = wide.t[:, :].rearrange("p (r n) -> p r n", r=2)
            else:
                view = lambda t: t[:, :].rearrange("p (z n) -> p z n", z=2)[:, nibble, :]
                src = wide.t[:, :]
            wide.last_use = b.split(view(slot.t[0]), view(slot.t[1]), src, b.act, b.pool, "s_weight", [m])
            marks += wide.last_use
            if nibble == 1:
                packed.last_use = scale.last_use = [m]

        return [bits, over, both, total, signed]

    def chores(self, n):
        for _ in range(min(n, len(self.waiting))):
            self.waiting.pop(0)()

    def gate_up(self, ch, beside):
        b = self.b
        cols = slice(ch * CT, (ch + 1) * CT)
        xh, xl = (t[:, :, cols] for t in self.xT)
        self.inters = []
        for z in range(2):
            beside()
            psums = []
            for k, name in enumerate(("s_gate", "s_up")):
                slot, ready = self.current[k]
                wh, wl = (t[:, :].rearrange("p (c n) -> p c n", c=DC) for t in slot.t)
                bank = b.banks.next()
                b.pe.wait(*bank.last_use)
                b.pe.wait(*ready, *self.x_ready[ch])
                ns = slice(z * P, (z + 1) * P)
                m = b.matmul3(bank.t[:, 0:CT], [(wh[:, c, ns], wl[:, c, ns], xh[:, c, :], xl[:, c, :]) for c in range(DC)],
                              b.count(name))
                slot.last_use = [m]
                psums.append((bank, bank.t[:, 0:CT], m))
            (gbank, g, mg), (ubank, u, mu) = psums
            sq, th, ac = self.sq.next(), self.tanh.next(), self.act.next()
            b.act.wait(*sq.last_use, mg)
            m = b.act.do(lambda e, o=sq.t, g=g: e.activation(o[:, :], g, ACT.Square), b.count("s_g2"))
            b.act.wait(m)
            m = b.act.do(lambda e, o=sq.t: e.activation(o[:, :], o[:, :], ACT.Copy, bias=GELU_C, scale=GELU_A * GELU_C),
                         b.count("s_poly"))
            b.dve.wait(m)
            m = b.dve.do(lambda e, o=sq.t, g=g: e.tensor_tensor(o[:, :], g, o[:, :], ALU.mult), b.count("s_arg"))
            b.act.wait(*th.last_use, m)
            m = b.act.do(lambda e, o=th.t, i=sq.t: e.activation(o[:, :], i[:, :], ACT.Tanh), b.count("s_tanh"))
            sq.last_use = [m]
            self.chores(5)
            b.dve.wait(*ac.last_use, m)
            m = b.dve.do(lambda e, o=ac.t, i=th.t, g=g: e.scalar_tensor_tensor(out=o[:, :], in0=i[:, :], scalar=1.0, in1=g,
                                                                              op0=ALU.add, op1=ALU.mult), b.count("s_gelu"))
            th.last_use = gbank.last_use = [m]
            b.dve.wait(m, mu)
            m = b.dve.do(lambda e, o=ac.t, u=u: e.scalar_tensor_tensor(out=o[:, :], in0=o[:, :], scalar=0.5, in1=u,
                                                                       op0=ALU.mult, op1=ALU.mult), b.count("s_inter"))
            ubank.last_use = [m]
            it = self.inter.next()
            b.act.wait(*it.last_use)
            b.pool.wait(*it.last_use)
            ac.last_use = b.split(it.t[0][:, :], it.t[1][:, :], ac.t[:, :], b.act, b.pool, "s_inters", [m])
            self.inters.append((it, ac.last_use))

    def down(self, ch, down, inters, last):
        b = self.b
        cols = slice(ch * CT, (ch + 1) * CT)
        slot, ready = down
        wh, wl = (t[:, :].rearrange("p (z n) -> p z n", z=2) for t in slot.t)
        b.pe.wait(*ready, *(m for _, r in inters for m in r))
        for c in range(DC):
            bank = b.banks.next()
            b.pe.wait(*bank.last_use)
            cs = slice(c * P, (c + 1) * P)
            m = b.matmul3(bank.t[:, 0:CT], [(wh[:, z, cs], wl[:, z, cs], inters[z][0].t[0][:, :], inters[z][0].t[1][:, :])
                                            for z in range(2)], b.count("s_down"))
            b.dve.wait(m, *self.y_done[ch])
            md = b.dve.do(lambda e, c=c, k=bank: e.tensor_tensor(self.yT[:, c, cols], k.t[:, 0:CT], self.yT[:, c, cols],
                                                                 ALU.add), b.count("s_yT_sum"))
            bank.last_use = [md]
        slot.last_use = [m]
        for it, _ in inters:
            it.last_use = [m]
        self.y_done[ch] = [md]
        if last:
            b.sp.wait(md)
            self.out_marks.append(b.sp.do(lambda e: e.dma_start(b.d["out"][:, :, cols], self.yT[:, :, cols]),
                                          b.count(f"d_out{ch}"), 16))

    def begin(self):
        b = self.b
        self.out_marks, self.building, self.waiting = [], [None] * 3, []
        for q in (b.act, b.dve, b.pool, b.sp):
            q.wait(*self.attention.units_done)
        self.fetch(0)
        self.load_x(0)
        self.pieces = [(k, n) for k in range(3) for n in range(2)]
        self.waiting = [f for k, n in self.pieces for f in self.decode(k, n)]
        return lambda: self.chores(5)

    def run(self):
        b = self.b
        b.banks.places = b.slow_banks.places + b.banks.places
        projected = [b.count(n).mark() for n in ("s_o", "s_oT_hi", "s_oT_lo", "s_out", "s_wv_hi", "s_wv_lo",
                                                 "s_headw_hi", "s_headw_lo")]
        for q in (b.act, b.dve, b.pool, b.sp):
            q.wait(*projected)
        self.chores(len(self.waiting))
        self.load_x(1)
        for ch in range(NCHUNK - 1):
            self.load_y(ch)
        prev = None
        for jt in range(JT):
            self.current = list(self.building)
            for ch in range(NCHUNK):
                if ch == 0 and jt + 1 < JT:
                    self.fetch(jt + 1)
                if ch == 1 and jt + 1 < JT:
                    self.waiting = [f for k, n in self.pieces for f in self.decode(k, n)]
                beside = self.attention.step if jt == 0 else lambda: None
                self.gate_up(ch, lambda: (beside(), beside()))
                step = (ch, self.current[2], self.inters, jt == JT - 1)
                if prev:
                    self.down(*prev)
                prev = step
                beside(), beside()
                if jt == 0:
                    if ch == 0:
                        self.load_x(2)
                    if ch == 1:
                        self.load_x(NCHUNK - 1)
                        self.load_y(NCHUNK - 1)
            self.chores(len(self.waiting))
        self.down(*prev)
        b.sp.wait(*self.out_marks)


def build(nc, d):
    with ExitStack() as ctx:
        b = Builder(nc, ctx, d)
        build_constants(b, ctx)
        with ExitStack() as s:
            attention = Attention(b, s, ctx)
        with ExitStack() as s:
            ffn = FeedForward(b, s, attention)
            attention.run(ffn)
            ffn.run()
            with nc.Block() as block:
                block.sync(b.sp.replay)
                block.tensor(b.pe.replay)
                block.scalar(b.act.replay)
                block.vector(b.dve.replay)
                block.gpsimd(b.pool.replay)


def kernel(**inputs):
    import concourse.bacc as bacc
    from concourse.bass_utils import run_bass_kernel_spmd

    a = {k: np.asarray(v) for k, v in inputs.items()}
    x, ctxs = a["x"], a["ctx_1024"]
    flat = x.reshape(TOKENS, DIM)

    def rows_by_byte(w):
        return w.reshape(JT, P, 2, 2, P).transpose(4, 0, 3, 2, 1).reshape(P, JT, 4 * P)

    def scales_by_block(w):
        return w.reshape(JT, P, 2, 2, 8).transpose(4, 0, 3, 2, 1).reshape(8, JT, 4 * P)

    arrays = {
        "x": x, "xT": flat.reshape(TOKENS, DC, P).transpose(2, 1, 0),
        "ctx": ctxs, "ctxT": ctxs.reshape(BATCH, SKV, CC, P).transpose(0, 3, 2, 1),
        "Wq": a["L0_xattn_Wq"], "Wk": a["L0_xattn_Wk"], "Wv": a["L0_xattn_Wv"], "Wo": a["L0_xattn_Wo"],
        "gq": a["L0_xattn_gq"].reshape(HD, 1), "gk": a["L0_xattn_gk"].reshape(HD, 1),
        "gate_packed": rows_by_byte(a["L0_ffn_gate_W_packed"]), "gate_scales": scales_by_block(a["L0_ffn_gate_scales"]),
        "up_packed": rows_by_byte(a["L0_ffn_up_W_packed"]), "up_scales": scales_by_block(a["L0_ffn_up_scales"]),
        "down_packed": a["L0_ffn_down_W_packed"].reshape(DIM, JT, P).transpose(2, 1, 0),
        "down_scales": a["L0_ffn_down_scales"].reshape(DIM, JT, 8).transpose(2, 1, 0),
    }
    arrays = {k: np.ascontiguousarray(v) for k, v in arrays.items()}
    nc = bacc.Bacc("TRN2", target_bir_lowering=False, num_devices=1)
    d = {k: nc.dram_tensor(f"in_{k}", v.shape, mybir.dt.from_np(v.dtype), kind="ExternalInput").ap()
         for k, v in arrays.items()}
    d["out"] = nc.dram_tensor("out_yT", (P, DC, TOKENS), F32, kind="ExternalOutput").ap()
    d["x1T"] = nc.dram_tensor("spill_x1T", (P, DC, TOKENS), F32, kind="Internal").ap()
    d["x2T"] = nc.dram_tensor("spill_x2T", (P, DC, TOKENS), F32, kind="Internal").ap()
    build(nc, d)
    r = run_bass_kernel_spmd(nc, [{f"in_{k}": v for k, v in arrays.items()}], core_ids=[0])
    out = r.results[0]["out_yT"]
    return out.transpose(2, 1, 0).reshape(BATCH, SQ, DIM)
```

```python
from contextlib import ExitStack

import numpy as np

import concourse.bass as bass
import concourse.mybir as mybir

F32 = mybir.dt.float32
F32R = mybir.dt.float32r
BF16 = mybir.dt.bfloat16
I32 = mybir.dt.int32
I16 = mybir.dt.int16
ALU = mybir.AluOpType
ACT = mybir.ActivationFunctionType
AX_X = mybir.AxisListType.X

P = 128
BATCH, SQ, DIM = 16, 100, 512
SKV, CDIM = 361, 256
HEADS, HD = 16, 128
MLP = 4096
FP4_BLOCK = 32
EPS = 1e-5
TOKENS = BATCH * SQ
BANK = 512
NBANKS = 8

GB = 4
NG = BATCH // GB
GT = GB * SQ
QH = 4
NQUAD = HEADS // QH
DC = DIM // P
CC = CDIM // P
KT = 3
KP = 122
KPAD = KT * KP
SCOLS = SKV + SKV % 2
LASTK = SKV - (KT - 1) * KP
UNITS = NG * NQUAD * GB

JT = MLP // (2 * P)
NCHUNK = 4
CT = TOKENS // NCHUNK
GELU_C = 0.7978845608028654
GELU_A = 0.044715


class Counter:

    def __init__(self, sem):
        self.sem, self.value = sem, 0

    def after(self, step):
        self.value += step
        return (self, self.value)

    def mark(self):
        return (self, self.value)


class Queue:

    def __init__(self):
        self.steps, self.seen = [], {}

    def wait(self, *marks):
        for counter, value in marks:
            if self.seen.get(counter, 0) < value:
                self.seen[counter] = value
                self.steps.append(lambda e, s=counter.sem, v=value: e.wait_ge(s, v))

    def do(self, emit, counter=None, step=1):
        if counter is None:
            self.steps.append(emit)
            return None
        self.steps.append(lambda e: emit(e).then_inc(counter.sem, step))
        return counter.after(step)

    def replay(self, engine):
        for s in self.steps:
            s(engine)


class Place:

    def __init__(self, t):
        self.t, self.last_use = t, []


class Turns:

    def __init__(self, tensors):
        self.places, self.n = [Place(t) for t in tensors], 0

    def next(self):
        self.n += 1
        return self.places[(self.n - 1) % len(self.places)]


class Builder:
    def __init__(self, nc, ctx, d):
        self.nc, self.ctx, self.d = nc, ctx, d
        self.pe, self.act, self.dve, self.pool, self.sp = (Queue() for _ in range(5))
        self.all_banks = [ctx.enter_context(nc.psum_tensor(f"bank{i}", [P, BANK], F32)) for i in range(NBANKS)]
        self.slow_banks, self.banks = Turns(self.all_banks[:KT]), Turns(self.all_banks[KT:])
        self.counters = {}

    def count(self, name):
        if name not in self.counters:
            self.counters[name] = Counter(self.ctx.enter_context(self.nc.semaphore(name)))
        return self.counters[name]

    def sb(self, stack, name, shape, dt=F32):
        return stack.enter_context(self.nc.sbuf_tensor(name, shape, dt))

    def all_marks(self):
        return [(c, c.value) for c in self.counters.values()]

    def matmul3(self, out, terms, counter):
        passes = [ab for lh, ll, rh, rl in terms for ab in ((lh, rh), (lh, rl), (ll, rh))]
        for i, (a, b) in enumerate(passes):
            first, last = i == 0, i == len(passes) - 1
            mark = self.pe.do(lambda e, a=a, b=b, f=first, l=last: e.matmul(out, a, b, start=f, stop=l),
                              counter if last else None)
        return mark

    def split(self, hi, lo, src, hi_engine, lo_engine, name, ready):
        hi_engine.wait(*ready)
        if hi_engine is self.act:
            m_hi = hi_engine.do(lambda e: e.copy(hi, src), self.count(name + "_hi"))
        else:
            m_hi = hi_engine.do(lambda e: e.tensor_scalar(hi, src, 1.0, 1.0, ALU.mult, ALU.mult),
                                self.count(name + "_hi"))
        lo_engine.wait(*ready, m_hi)
        m_lo = lo_engine.do(lambda e: e.tensor_tensor(lo, src, hi.bitcast(F32), ALU.subtract),
                            self.count(name + "_lo"))
        return [m_hi, m_lo]

    def load(self, dst, src, name, queue=None):
        return (queue or self.sp).do(lambda e: e.dma_start(dst, src), self.count(name), 16)


def build_constants(b, s):
    nc, d = b.nc, b.d
    b.ident = b.sb(s, "ident", [P, P])
    b.power = b.sb(s, "power", [P, QH * GB])
    b.selector_f = b.sb(s, "selector_f", [P, P])
    b.selector = b.sb(s, "selector", [P, QH, P], F32R)
    m = b.pool.do(lambda e: e.memset(b.ident[:, :], 0.0), b.count("s_const"))
    b.pool.wait(m)
    b.const = [b.pool.do(lambda e: e.affine_select(out=b.ident[:, :], in_=b.ident[:, :], compare_op=ALU.not_equal,
                                                   fill=1.0, base=0, pattern=[[-1, P]], channel_multiplier=1),
                         b.count("s_const"))]
    b.const.append(b.pool.do(lambda e: e.memset(b.power[:, :], -0.5), b.count("s_const")))
    m = b.pool.do(lambda e: e.memset(b.selector_f[:, :], 0.0), b.count("s_const"))
    for h in range(QH):
        b.pool.wait(m)
        b.pool.do(lambda e, h=h: e.memset(b.selector_f[:, h:h + 1], 1.0), b.count("s_const"))
        b.pool.wait(b.count("s_const").mark())
        m = b.pool.do(lambda e, h=h: e.tensor_copy(b.selector[:, h, :], b.selector_f[:, :]), b.count("s_const"))
        b.pool.wait(m)
        m = b.pool.do(lambda e, h=h: e.memset(b.selector_f[:, h:h + 1], 0.0), b.count("s_const"))
    b.const.append(m)


class Attention:
    def __init__(self, b, s, lasting):
        self.b = b
        sb = lambda name, shape, dt=F32: b.sb(s, name, shape, dt)
        pair = lambda name, shape: (sb(name + "_hi", shape, F32R), sb(name + "_lo", shape, F32R))
        sl = lambda name, shape: b.sb(lasting, name, shape)
        self.gqk = sl("gqk", [P, 3])
        self.x_raw = Place(sl("x_raw", [SQ, DIM]))
        self.x_norm = Turns([sl(f"x_norm{i}", [SQ, DIM]) for i in range(2)])
        self.ln_small = Turns([sl(f"ln_small{i}", [SQ, 12]) for i in range(2)])
        self.x1T = Place(sl("x1T", [P, DC, GT]))
        self.x1T_done = []
        self.x2T = Place(sl("x2T", [P, DC * SQ]))
        self.x2_spilled = [[] for _ in range(NG)]
        self.x1_spilled = [[] for _ in range(NG)]
        self.ctxT = [pair(f"ctxT{i}", [P, CC, KPAD]) for i in range(GB)]
        self.ctxN = [pair(f"ctxN{i}", [KP, KT, CDIM]) for i in range(GB)]
        self.ctxT_ready, self.ctxT_used, self.ctxN_ready, self.ctxN_used = ([[] for _ in range(GB)] for _ in range(4))
        self.ctxT_raw = Place(sb("ctxT_raw", [P, CC, KPAD]))
        self.ctxN_raw = Place(sb("ctxN_raw", [KP, KT, CDIM]))
        self.xlnT = pair("xlnT", [P, DC, GT])
        self.xlnT_used, self.xlnT_ready = [], []
        self.qT = [pair(f"qT{h}", [P, GT]) for h in range(QH)]
        self.qT_used, self.qT_ready = [[] for _ in range(QH)], [[] for _ in range(QH)]
        self.queries_tail, self.q_var_ready = None, None
        self.q_sq = Place(sb("q_sq", [P, GT]))
        self.q_sq_split = Turns([pair(f"q_sq{i}", [P, GT]) for i in range(2)])
        self.q_var = Place(sb("q_var", [QH, GT]))
        self.q_rstd = Turns([sb(f"q_rstd{i}", [SQ, GB * QH]) for i in range(2)])
        self.wk, self.wk_raw = pair("wk", [P, CC, QH * HD]), Place(sb("wk_raw", [P, CC, QH * HD]))
        self.wk_used = []
        self.k_sq = Turns([sb(f"k_sq{i}", [KP, QH * HD]) for i in range(1)])
        self.k_ss = Turns([sb(f"k_ss{i}", [KP, KT * QH]) for i in range(2)])
        self.khat = Place(sb("khat", [KP, KT, QH * HD]))
        self.kT = pair("kT", [P, QH, KPAD])
        self.kT_used, self.kT_ready = [], []
        self.attn = [Place(sb(f"attn{h}", [SQ, KPAD])) for h in range(QH)]
        self.stats = Turns([sb(f"stats{i}", [SQ, 3 * QH]) for i in range(2)])
        self.aT = pair("aT", [KP, KT, QH * SQ])
        self.aT_used, self.aT_ready = [], []
        self.yT = pair("yT", [P, CC, QH, GT])
        self.yT_used, self.yT_ready = [], []
        self.oT = Turns([pair(f"oT{i}", [P, GT]) for i in range(2)])
        self.head_w = Turns([pair(f"head_w{i}", [P, DIM]) for i in range(3)])
        self.head_raw = Turns([sb(f"head_raw{i}", [P, DIM]) for i in range(2)])
        self.wv_ring = Turns([pair(f"wv{i}", [P, CC * HD]) for i in range(2)])
        self.wv_raw = Turns([sb(f"wv_raw{i}", [P, CC * HD]) for i in range(2)])
        self.head_queue, self.wv_queue = [], []

    def setup(self):
        b = self.b
        self.pads = [b.dve.do(lambda e: e.memset(self.ctxT_raw.t[:, :, SKV:KPAD], 0.0), b.count("s_pad")),
                     b.dve.do(lambda e: e.memset(self.ctxN_raw.t[LASTK // 32 * 32:KP, KT - 1, :], 0.0),
                              b.count("s_pad"))]
        for h in range(QH):
            self.pads.append(b.dve.do(lambda e, h=h: e.memset(self.attn[h].t[:, SKV:KPAD], 0.0), b.count("s_pad")))
        m = [b.load(self.gqk[:, 0:1], b.d["gq"], "d_gq"), b.load(self.gqk[:, 1:2], b.d["gk"], "d_gk")]
        b.dve.wait(*m)
        self.gqk_ready = b.dve.do(lambda e: e.scalar_tensor_tensor(
            out=self.gqk[:, 2:3], in0=self.gqk[:, 0:1], scalar=float(HD) ** -0.5, in1=self.gqk[:, 1:2],
            op0=ALU.mult, op1=ALU.mult), b.count("s_gqk"))

    def load_ctxT(self, batch, hi_engine=None, lo_engine=None):
        b, i, raw = self.b, batch % GB, self.ctxT_raw
        b.sp.wait(*self.pads, *raw.last_use)
        m = b.load(raw.t[:, :, 0:SKV], b.d["ctxT"][batch], "d_ctxT")
        tag = "_first" if hi_engine else ""
        hi_engine, lo_engine = hi_engine or b.pool, lo_engine or b.pool
        for q in {hi_engine, lo_engine}:
            q.wait(*self.ctxT_used[i])
        hi, lo = self.ctxT[i]
        raw.last_use = self.ctxT_ready[i] = b.split(hi[:, :, :], lo[:, :, :], raw.t[:, :, :], hi_engine, lo_engine,
                                                    "s_ctxT" + tag, [m])

    def load_ctxN(self, batch):
        b, i, raw = self.b, batch % GB, self.ctxN_raw
        b.sp.wait(*self.pads, *raw.last_use)
        m = [b.load(raw.t[:, 0:KT - 1, :],
                    b.d["ctx"][batch, 0:(KT - 1) * KP, :].rearrange("(t p) c -> p t c", p=KP), "d_ctxN"),
             b.load(raw.t[0:LASTK, KT - 1, :], b.d["ctx"][batch, (KT - 1) * KP:SKV, :], "d_ctxN2")]
        b.pool.wait(*self.ctxN_used[i])
        hi, lo = self.ctxN[i]
        raw.last_use = self.ctxN_ready[i] = b.split(hi[:, :, :], lo[:, :, :], raw.t[:, :, :], b.pool, b.pool, "s_ctxN", m)

    def fetch_wk(self, quad):
        b = self.b
        b.sp.wait(*self.wk_raw.last_use)
        src = b.d["Wk"][:, quad * QH * HD:(quad + 1) * QH * HD].rearrange("(c p) n -> p c n", p=P)
        self.wk_fetched = b.load(self.wk_raw.t[:, :, :], src, "d_wk")

    def split_wk(self, hi_engine, lo_engine, name):
        b = self.b
        for q in {hi_engine, lo_engine}:
            q.wait(*self.wk_used)
        self.wk_ready = b.split(self.wk[0][:, :, :], self.wk[1][:, :, :], self.wk_raw.t[:, :, :],
                                hi_engine, lo_engine, name, [self.wk_fetched])
        self.wk_raw.last_use = self.wk_ready

    def load_head_weight(self, kind, head):
        b = self.b
        raw = self.head_raw.next()
        b.sp.wait(*raw.last_use)
        if kind == "q":
            src = b.d["Wq"][:, head * HD:(head + 1) * HD].rearrange("(c p) n -> p c n", p=P)
            dst = raw.t[:, :].rearrange("p (c n) -> p c n", c=DC)
        else:
            src, dst = b.d["Wo"][head * HD:(head + 1) * HD, :], raw.t[:, :]
        m = b.load(dst, src, f"d_head{self.head_raw.n % 2}")
        slot = self.head_w.next()
        b.pool.wait(*slot.last_use)
        raw.last_use = b.split(slot.t[0][:, :], slot.t[1][:, :], raw.t[:, :], b.pool, b.pool, "s_headw", [m])
        self.head_queue.append((slot, raw.last_use))

    def load_wv(self, head):
        b = self.b
        raw = self.wv_raw.next()
        b.sp.wait(*raw.last_use)
        src = b.d["Wv"][:, head * HD:(head + 1) * HD].rearrange("(c p) n -> p c n", p=P)
        m = b.load(raw.t[:, :].rearrange("p (c n) -> p c n", c=CC), src, f"d_wv{self.wv_raw.n % 2}")
        slot = self.wv_ring.next()
        b.pool.wait(*slot.last_use)
        raw.last_use = b.split(slot.t[0][:, :], slot.t[1][:, :], raw.t[:, :], b.pool, b.pool, "s_wv", [m])
        self.wv_queue.append((slot, raw.last_use))

    def moments(self, src, ready):
        b = self.b
        small = self.ln_small.next()
        st = small.t
        b.dve.wait(*small.last_use, *ready)
        m = b.dve.do(lambda e: e.bn_stats(st[:, 0:6], src), b.count("s_bn"))
        b.dve.wait(m)
        m = b.dve.do(lambda e: e.bn_aggr(st[:, 6:8], st[:, 0:6]), b.count("s_bn"))
        b.dve.wait(m)
        m = b.dve.do(lambda e: e.tensor_scalar(st[:, 8:9], st[:, 7:8], EPS, None, ALU.add), b.count("s_bn"))
        b.pool.wait(m, *b.const)
        m = b.pool.do(lambda e: e.tensor_tensor(st[:, 9:10], st[:, 8:9], b.power[0:SQ, 0:1], ALU.pow),
                      b.count("s_lnrstd"))
        return small, m

    def normalise(self, src, moments):
        b = self.b
        small, m = moments
        st, norm = small.t, self.x_norm.next()
        b.dve.wait(m, *norm.last_use)
        m = b.dve.do(lambda e: e.tensor_scalar(norm.t[:, :], src, st[:, 6:7], st[:, 9:10], ALU.subtract, ALU.mult),
                     b.count("s_xnorm"))
        small.last_use = [m]
        return norm, m

    def norm_transposed(self, norm, ready, parity):
        b = self.b
        bank = b.banks.next()
        b.pe.wait(*bank.last_use)
        b.pe.wait(ready, *b.const)
        for c in range(DC):
            if parity:
                lo = (c // 2) * 2 * P + c % 2
                src = norm.t[:, lo:lo + 2 * P - 1:2]
            else:
                src = norm.t[:, c * P:(c + 1) * P]
            m = b.pe.do(lambda e, c=c, src=src: e.transpose(bank.t[:, c * SQ:(c + 1) * SQ], src, b.ident[0:SQ, 0:SQ]),
                        b.count("s_normT") if c == DC - 1 else None)
        norm.last_use = [m]
        return bank, m

    def load_tokens(self, batch):
        self.b.sp.wait(*self.x_raw.last_use)
        self.x_loaded = self.b.load(self.x_raw.t[:, :], self.b.d["x"][batch], "d_x")

    def ln1(self, batch):
        b, i, kept = self.b, batch % GB, {}

        def first():
            kept["moments"] = self.moments(self.x_raw.t[:, :], [self.x_loaded])

        def second():
            kept["norm"] = self.normalise(self.x_raw.t[:, :], kept["moments"])
            self.x_raw.last_use = [kept["norm"][1]]

        def third():
            bank, m = self.norm_transposed(*kept["norm"], False)
            if i == 0:
                b.act.wait(*self.xlnT_used)
                b.dve.wait(*self.xlnT_used)
                self.xlnT_used, self.xlnT_ready = [], []
            cols = slice(i * SQ, (i + 1) * SQ)
            bank.last_use = b.split(self.xlnT[0][:, :, cols], self.xlnT[1][:, :, cols],
                                    bank.t[:, 0:DC * SQ].rearrange("p (c n) -> p c n", c=DC), b.act, b.dve, "s_xlnT", [m])
            self.xlnT_ready += bank.last_use

        return [first, second, third]

    def queries(self, loads):
        b = self.b
        xh, xl = self.xlnT
        sbank = b.banks.next()
        b.pe.wait(*sbank.last_use)
        ssum = sbank.t[:, 0:GT]
        squares = []

        def add_squares(h):
            place, ready = squares[h]
            b.pe.wait(*ready, *b.const)
            for k in range(2):
                m = b.pe.do(lambda e, k=k: e.matmul(ssum, b.selector[:, h, :], place.t[k][:, :],
                                                    start=h == 0 and k == 0, stop=h == QH - 1 and k == 1),
                            b.count("s_qss") if k else None)
            place.last_use = [m]
            return m

        for h in range(QH):
            slot, wready = self.head_queue.pop(0)
            wh, wl = slot.t
            bank = b.slow_banks.next()
            b.pe.wait(*bank.last_use)
            b.pe.wait(*wready, *self.xlnT_ready)
            q = bank.t[:, 0:GT]
            m = b.matmul3(q, [(wh[:, c * HD:(c + 1) * HD], wl[:, c * HD:(c + 1) * HD], xh[:, c, :], xl[:, c, :])
                              for c in range(DC)], b.count("s_q"))
            slot.last_use = self.xlnT_used = [m]
            b.act.wait(m, *self.q_sq.last_use)
            m2 = b.act.do(lambda e, q=q: e.activation(self.q_sq.t[:, :], q, ACT.Square), b.count("s_qsq"))
            place = self.q_sq_split.next()
            b.act.wait(*place.last_use)
            b.dve.wait(*place.last_use)
            sh, sl = place.t
            ready = self.q_sq.last_use = b.split(sh[:, :], sl[:, :], self.q_sq.t[:, :], b.act, b.dve, "s_qsqs", [m2])
            b.act.wait(*self.qT_used[h], self.gqk_ready)
            b.dve.wait(*self.qT_used[h])
            qh, ql = self.qT[h]
            m3 = b.act.do(lambda e, q=q, o=qh: e.activation(o[:, :], q, ACT.Copy, scale=self.gqk[:, 2:3]), b.count("s_qT_hi"))
            b.dve.wait(m3)
            m4 = b.dve.do(lambda e, q=q, o=ql, hi=qh: e.scalar_tensor_tensor(
                out=o[:, :], in0=q, scalar=self.gqk[:, 2:3], in1=hi[:, :].bitcast(F32), op0=ALU.mult, op1=ALU.subtract),
                b.count("s_qT_lo"))
            bank.last_use = [m2, m4]
            self.qT_ready[h], self.qT_used[h] = [m3, m4], []
            squares.append((place, ready))
            if h > 0:
                add_squares(h - 1)
            self.load_head_weight(*loads[h])
        self.queries_tail = (add_squares, sbank, ssum)

    def queries_squares(self):
        if self.queries_tail is None:
            return
        b = self.b
        add_squares, sbank, ssum = self.queries_tail
        self.queries_tail = None
        m = add_squares(QH - 1)
        b.dve.wait(m, *self.q_var.last_use)
        m = b.dve.do(lambda e: e.tensor_scalar(self.q_var.t[:, :], ssum[0:QH, :], 1.0 / HD, EPS, ALU.mult, ALU.add),
                     b.count("s_qvar"))
        sbank.last_use = [m]
        self.q_var_ready = m

    def queries_rstd(self):
        if self.q_var_ready is None:
            return
        b, m = self.b, self.q_var_ready
        self.q_var_ready = None
        bank = b.banks.next()
        b.pe.wait(*bank.last_use)
        b.pe.wait(m)
        for i in range(GB):
            m = b.pe.do(lambda e, i=i: e.transpose(bank.t[0:SQ, i * QH:(i + 1) * QH], self.q_var.t[:, i * SQ:(i + 1) * SQ],
                                                   b.ident[0:QH, 0:QH]), b.count("s_qvarT") if i == GB - 1 else None)
        self.q_var.last_use = [m]
        rstd = self.q_rstd.next()
        b.dve.wait(m, *rstd.last_use)
        m = b.dve.do(lambda e: e.tensor_copy(rstd.t[:, :], bank.t[0:SQ, 0:GB * QH]), b.count("s_qvarT_sb"))
        bank.last_use = [m]
        b.pool.wait(m, *b.const)
        m = b.pool.do(lambda e: e.tensor_tensor(rstd.t[:, :], rstd.t[:, :], b.power[0:SQ, 0:GB * QH], ALU.pow),
                      b.count("s_qrstd"))
        self.rstd_q, self.rstd_q_ready = rstd, m

    def keys(self, unit, tiles, sums=True):
        b, i = self.b, unit % GB
        if 0 in tiles:
            self.k_tiles, self.khat_ready = [], []
            self.k_rstd = self.k_ss.next()
        th, tl = self.ctxT[i]
        wh, wl = self.wk
        b.pe.wait(*self.ctxT_ready[i], *self.wk_ready)
        for t in tiles:
            bank = b.slow_banks.next()
            b.pe.wait(*bank.last_use)
            ks = slice(t * KP, (t + 1) * KP)
            m = b.matmul3(bank.t[0:KP, :], [(th[:, c, ks], tl[:, c, ks], wh[:, c, :], wl[:, c, :]) for c in range(CC)],
                          b.count("s_k"))
            self.wk_used = self.ctxT_used[i] = [m]
            sq = self.k_sq.next()
            b.act.wait(m, *sq.last_use)
            m = b.act.do(lambda e, s=sq, k=bank: e.activation(s.t[:, :], k.t[0:KP, :], ACT.Square), b.count("s_ksq"))
            self.k_tiles.append((bank, sq, m))
            if sums:
                self.key_sums(t)

    def key_sums(self, t):
        b, ss = self.b, self.k_rstd
        bank, sq, m = self.k_tiles[t]
        cols = ss.t[:, t * QH:(t + 1) * QH]
        b.dve.wait(m, *ss.last_use)
        m = b.dve.do(lambda e: e.tensor_reduce(cols, sq.t[:, :].rearrange("p (h d) -> p h d", h=QH), AX_X, ALU.add),
                     b.count("s_kss"))
        sq.last_use = [m]
        b.pool.wait(m, *b.const)
        m = b.pool.do(lambda e: e.tensor_scalar(cols, cols, 1.0 / HD, EPS, ALU.mult, ALU.add), b.count("s_kvar"))
        b.pool.wait(m)
        m = b.pool.do(lambda e: e.tensor_tensor(cols, cols, b.power[0:KP, 0:QH], ALU.pow), b.count("s_krstd"))
        self.k_tiles[t] = (bank, sq, m)

    def normalise_keys(self, tiles):
        b, ss = self.b, self.k_rstd
        for t in tiles:
            bank, _, m = self.k_tiles[t]
            b.dve.wait(m, *self.khat.last_use)
            m = b.dve.do(lambda e, t=t, k=bank: e.tensor_tensor(
                self.khat.t[:, t, :].rearrange("p (h d) -> p h d", h=QH),
                k.t[0:KP, :].rearrange("p (h d) -> p h d", h=QH),
                ss.t[:, t * QH:(t + 1) * QH].unsqueeze(2).broadcast_to([KP, QH, HD]), ALU.mult), b.count("s_khat"))
            bank.last_use = [m]
            self.khat_ready.append(m)
            ss.last_use = [m]

    def transpose_keys(self):
        b = self.b
        b.pe.wait(*b.const)
        b.act.wait(*self.kT_used)
        b.dve.wait(*self.kT_used)
        self.kT_ready = []
        kh, kl = self.kT
        for t in range(KT):
            bank = b.banks.next()
            b.pe.wait(self.khat_ready[t], *bank.last_use)
            for h in range(QH):
                m = b.pe.do(lambda e, t=t, h=h, k=bank: e.transpose(
                    k.t[:, h * KP:(h + 1) * KP], self.khat.t[:, t, h * HD:(h + 1) * HD], b.ident[0:KP, 0:KP]),
                    b.count("s_kTp") if h == QH - 1 else None)
            ks = slice(t * KP, (t + 1) * KP)
            bank.last_use = b.split(kh[:, :, ks], kl[:, :, ks], bank.t[:, 0:QH * KP].rearrange("p (h n) -> p h n", h=QH),
                                   b.act, b.dve, "s_kT", [m])
            self.kT_ready += bank.last_use
            self.khat.last_use = [m]
            if t == 0:
                self.queries_rstd()

    def scores(self, unit, between_maxima, before_sums, between):
        b, i = self.b, unit % GB
        st = self.stats.next()
        b.dve.wait(*st.last_use)
        neg, total, inv = (st.t[:, k * QH:(k + 1) * QH] for k in range(3))
        rq = self.rstd_q.t
        b.act.wait(*self.pads)
        maxima, exps, self.attn_ready = [], [], []

        def exponentials(h):
            bank, m = maxima[h]
            col = slice(i * QH + h, i * QH + h + 1)
            b.dve.wait(m, self.rstd_q_ready)
            m = b.dve.do(lambda e: e.tensor_tensor(neg[:, h:h + 1], neg[:, h:h + 1], rq[:, col], ALU.mult),
                         b.count("s_negmax"))
            b.act.wait(m, *self.attn[h].last_use)
            exps.append(b.act.do(lambda e: e.activation(
                self.attn[h].t[:, 0:SKV], bank.t[0:SQ, 0:SKV], ACT.Exp, bias=neg[:, h:h + 1], scale=rq[:, col],
                accum_out=total[:, h:h + 1]), b.count("s_exp")))
            bank.last_use = [exps[h]]

        def inverse(first, last):
            b.dve.wait(exps[last])
            return b.dve.do(lambda e: e.reciprocal(inv[:, first:last + 1], total[:, first:last + 1]), b.count("s_inv"))

        for h in range(QH):
            bank = b.banks.next()
            b.pe.wait(*bank.last_use)
            qs = slice(i * SQ, (i + 1) * SQ)
            (qh, ql), (kh, kl) = self.qT[h], self.kT
            b.pe.wait(*self.kT_ready, *self.qT_ready[h])
            m = b.matmul3(bank.t[0:SQ, 0:SCOLS], [(qh[:, qs], ql[:, qs], kh[:, h, 0:SCOLS], kl[:, h, 0:SCOLS])],
                          b.count("s_sc"))
            self.kT_used, self.qT_used[h] = [m], [m]
            b.dve.wait(m)
            m2 = b.dve.do(lambda e, h=h, k=bank: e.tensor_reduce(neg[:, h:h + 1], k.t[0:SQ, 0:SKV], AX_X, ALU.max,
                                                                 negate=True), b.count("s_max"))
            maxima.append((bank, m2))
            if h > 0:
                exponentials(h - 1)
            if h == 2:
                between_maxima()
        exponentials(QH - 1)
        before_sums()
        inverses = [inverse(h, h) for h in range(QH // 2)]
        for h, m in enumerate(inverses):
            b.dve.wait(m)
            self.attn_ready.append(b.dve.do(lambda e, h=h: e.tensor_scalar(
                self.attn[h].t[:, 0:SKV], self.attn[h].t[:, 0:SKV], inv[:, h:h + 1], None, ALU.mult), b.count("s_attn")))
        between()
        self.inverse_rest = inverse(QH // 2, QH - 1)
        self.rstd_q.last_use = exps
        self.stats_now = st

    def normalise_rest(self):
        b, st = self.b, self.stats_now
        b.act.wait(self.inverse_rest)
        for h in range(QH // 2, QH):
            self.attn_ready.append(b.act.do(lambda e, h=h: e.activation(
                self.attn[h].t[:, 0:SKV], self.attn[h].t[:, 0:SKV], ACT.Copy, scale=st.t[:, 2 * QH + h:2 * QH + h + 1]),
                b.count("s_attn_rest")))
        st.last_use = [self.attn_ready[QH // 2 - 1], self.attn_ready[-1]]

    def transpose_attn(self, between):
        b = self.b
        ah, al = self.aT
        b.act.wait(*self.aT_used)
        b.dve.wait(*self.aT_used)
        self.aT_used, self.aT_ready = [], []
        banks = [b.banks.next() for _ in range(KT)]
        for bank in banks:
            b.pe.wait(*bank.last_use)
        for h in range(QH):
            b.pe.wait(self.attn_ready[h])
            for t, bank in enumerate(banks):
                m = b.pe.do(lambda e, t=t, h=h, k=bank: e.transpose(
                    k.t[0:KP, h * SQ:(h + 1) * SQ], self.attn[h].t[:, t * KP:(t + 1) * KP], b.ident[0:SQ, 0:SQ]),
                    b.count("s_aTp"))
            self.attn[h].last_use = [m]
        between()
        for t, bank in enumerate(banks):
            bank.last_use = b.split(ah[:, t, :], al[:, t, :], bank.t[0:KP, 0:QH * SQ], b.act, b.dve, "s_aT", [m])
            self.aT_ready += bank.last_use

    def attend(self, unit):
        b, i = self.b, unit % GB
        (ah, al), (nh, nl), (yh, yl) = self.aT, self.ctxN[i], self.yT
        b.pe.wait(*self.aT_ready, *self.ctxN_ready[i])
        if i == 0:
            b.act.wait(*self.yT_used)
            b.dve.wait(*self.yT_used)
            self.yT_used, self.yT_ready = [], []
        for c in range(CC):
            bank = b.banks.next()
            b.pe.wait(*bank.last_use)
            cs = slice(c * P, (c + 1) * P)
            m = b.matmul3(bank.t[:, 0:QH * SQ], [(nh[:, t, cs], nl[:, t, cs], ah[:, t, :], al[:, t, :]) for t in range(KT)],
                          b.count("s_y"))
            qs = slice(i * SQ, (i + 1) * SQ)
            bank.last_use = b.split(yh[:, c, :, qs], yl[:, c, :, qs],
                                   bank.t[:, 0:QH * SQ].rearrange("p (h n) -> p h n", h=QH), b.act, b.dve, "s_yT", [m])
            self.yT_ready += bank.last_use
        self.aT_used = [m]
        self.ctxN_used[i] = [m]

    def project(self, group, quad, weights, beside, last):
        b = self.b
        if quad == 0:
            b.sp.wait(*self.x1T.last_use)
            m = b.load(self.x1T.t[:, :, :], b.d["xT"][:, :, group * GT:(group + 1) * GT], "d_xT")
            self.x1T_done = [m]
        yh, yl = self.yT
        heads = []

        def value(h):
            slot, wready = self.wv_queue.pop(0)
            wh, wl = slot.t
            bank = b.slow_banks.next()
            b.pe.wait(*bank.last_use)
            b.pe.wait(*wready, *self.yT_ready)
            m = b.matmul3(bank.t[:, 0:GT], [(wh[:, c * HD:(c + 1) * HD], wl[:, c * HD:(c + 1) * HD],
                                             yh[:, c, h, :], yl[:, c, h, :]) for c in range(CC)], b.count("s_o"))
            slot.last_use = [m]
            self.yT_used = [m]
            o = self.oT.next()
            b.act.wait(*o.last_use)
            b.dve.wait(*o.last_use)
            bank.last_use = b.split(o.t[0][:, :], o.t[1][:, :], bank.t[:, 0:GT], b.act, b.dve, "s_oT", [m])
            heads.append((o, bank.last_use))
            if h + 2 < QH:
                self.load_wv(quad * QH + h + 2)

        value(0)
        value(1)
        if last:
            last()
        beside()
        outs = [b.banks.next() for _ in range(DC)]
        for bank in outs:
            b.pe.wait(*bank.last_use)
        for h in range(QH):
            slot, wready = self.head_queue.pop(0)
            wh, wl = slot.t
            o, oready = heads[h]
            b.pe.wait(*wready, *oready)
            for c in range(DC):
                cs = slice(c * P, (c + 1) * P)
                out = outs[c].t[:, 0:GT]
                for k, (a, r) in enumerate(((wh, o.t[0]), (wh, o.t[1]), (wl, o.t[0]))):
                    f, l = h == 0 and k == 0, h == QH - 1 and k == 2
                    m = b.pe.do(lambda e, out=out, a=a, r=r, cs=cs, f=f, l=l: e.matmul(
                        out, a[:, cs], r[:, :], start=f, stop=l),
                        b.count("s_out") if k == 2 and (c == DC - 1 or h == QH - 1) else None)
                if h == QH - 1:
                    b.dve.wait(m, *self.x1T_done)
                    md = b.dve.do(lambda e, c=c, out=out: e.tensor_tensor(self.x1T.t[:, c, :], out, self.x1T.t[:, c, :],
                                                                          ALU.add), b.count("s_x1T"))
                    outs[c].last_use = [md]
            slot.last_use = [m]
            o.last_use = [m]
            if h + 2 < QH:
                value(h + 2)
            beside()
            if weights:
                self.load_head_weight(*weights.pop(0))
        self.x1T_done = [md]

    def spill_x1(self, group):
        b = self.b
        b.sp.wait(*self.x1T_done)
        self.x1_spilled[group] = [b.sp.do(
            lambda e: e.dma_start(b.d["x1T"][:, :, group * GT:(group + 1) * GT], self.x1T.t[:, :, :]), b.count("d_x1T_out"), 16)]
        self.x1T.last_use = list(self.x1_spilled[group])

    def ln2(self, group, j):
        b, kept = self.b, {}

        def first():
            bank = b.banks.next()
            b.pe.wait(*bank.last_use)
            b.pe.wait(*self.x1T_done)
            for c in range(DC):
                m = b.pe.do(lambda e, c=c: e.transpose(
                    bank.t[0:SQ, c * P:(c + 1) * P], self.x1T.t[:, c, j * SQ:(j + 1) * SQ], b.ident[:, :]),
                    b.count("s_x1") if c == DC - 1 else None)
            self.x1T.last_use = self.x1T.last_use + [m]
            kept["bank"], kept["moments"] = bank, self.moments(bank.t[0:SQ, :], [m])
            bank.last_use = None

        def second():
            kept["norm"] = self.normalise(kept["bank"].t[0:SQ, :], kept["moments"])
            kept["bank"].last_use = [kept["norm"][1]]

        def third():
            bank, m = self.norm_transposed(*kept["norm"], True)
            b.act.wait(m, *self.x2T.last_use)
            m = b.act.do(lambda e: e.copy(self.x2T.t[:, :], bank.t[:, 0:DC * SQ]), b.count("s_x2T"))
            bank.last_use = [m]
            b.sp.wait(m)
            cols = slice(group * GT + j * SQ, group * GT + (j + 1) * SQ)
            m = b.sp.do(lambda e: e.dma_start(b.d["x2T"][:, :, cols], self.x2T.t[:, :].rearrange("p (c n) -> p c n", c=DC)),
                        b.count("d_x2T_out"), 16)
            self.x2T.last_use = [m]
            self.x2_spilled[group].append(m)

        return [first, second, third]

    def step(self):
        if self.steps:
            self.steps.pop(0)()

    def steps_on(self):
        for _ in range(2 if len(self.steps) % 3 == 0 else 3):
            self.step()

    def run(self, feed_forward):
        b = self.b
        self.steps = []
        self.setup()
        early = (b.act, b.dve)
        norms = [self.ln1(i) for i in range(GB)]
        self.load_tokens(0)
        norms[0][0]()
        self.fetch_wk(0)
        self.load_ctxT(0, *early)
        norms[0][1]()
        self.load_tokens(1)
        self.split_wk(*early, "s_wk_first")
        norms[1][0]()
        self.keys(0, range(KT))
        norms[0][2]()
        norms[1][1]()
        for i in range(2, GB):
            self.load_tokens(i)
            norms[i][0]()
            norms[i - 1][2]()
            norms[i][1]()
            self.load_head_weight("q", i - 2)
        norms[GB - 1][2]()
        self.load_head_weight("q", 2)
        self.load_ctxT(1)
        self.load_ctxN(0)
        self.normalise_keys(range(KT))
        self.queries([("q", 3 + h) for h in range(QH)])
        self.queries_squares()
        self.queries_rstd()
        self.load_ctxN(1)
        for i in range(2, GB):
            self.load_ctxT(i)
            self.load_ctxN(i)
        pending, beside = None, lambda: None
        for u in range(UNITS + 1):
            group, quad, i = u // (NQUAD * GB), u // GB % NQUAD, u % GB
            last_quad, qn = quad == NQUAD - 1, u // GB + 1
            if u < UNITS:
                ahead = i + 1 - GB * (NQUAD - 1 - quad)
                if ahead in range(GB) and group + 1 < NG:
                    self.steps += self.ln1((group + 1) * GB + ahead)
                elif quad == 0 and group > 0 and i > 0:
                    for j in (range(i - 1, i) if i < 3 else range(2, GB)):
                        self.steps += self.ln2(group - 1, j)
                if u + 1 == UNITS:
                    feed_forward.begin_codes()
                self.transpose_keys()
                if u + 1 < UNITS:
                    self.keys(u + 1, [0])
                self.step()
                if u + 1 < UNITS:
                    self.keys(u + 1, [1], sums=False)
                if i == 1:
                    for h in range(2):
                        self.load_wv(quad * QH + h)
                elif last_quad and i == GB - 1 and group + 1 < NG:
                    self.load_ctxT((group + 1) * GB + 1)
                    self.load_ctxN((group + 1) * GB + 1)
                elif quad == 0 and group > 0 and i == 0:
                    self.load_ctxT(group * GB + 2)
                    self.load_ctxN(group * GB + 2)
                self.scores(u, lambda: self.key_sums(1) if u + 1 < UNITS else None, self.step,
                            lambda: self.normalise_keys([0] if u + 1 < UNITS else []))
                if u + 1 < UNITS:
                    self.keys(u + 1, [2])
                    self.normalise_keys([1])
                self.normalise_rest()
            if u > 0:
                self.attend(u - 1)
            if i == 2 and qn < NG * NQUAD:
                self.split_wk(b.act, b.pool, "s_wk")
            if u < UNITS:
                if u + 1 < UNITS:
                    self.normalise_keys([2])
                    if i == GB - 1:
                        self.queries([("q", qn % NQUAD * QH + 3)] + [("o", quad * QH + h) for h in range(3)])
                self.step()
                self.transpose_attn(self.queries_squares)
                if u + 1 == UNITS:
                    feed_forward.begin()
                    feed_forward.chores(6)
            else:
                self.units_done = b.all_marks()
                beside = lambda: feed_forward.chores(6)
            if ahead + 1 in range(GB) and group + 1 < NG:
                self.load_tokens((group + 1) * GB + ahead + 1)
            if last_quad and i == 1 and group + 1 < NG:
                self.load_ctxT((group + 1) * GB)
                self.load_ctxN((group + 1) * GB)
            if pending is not None:
                g, q = pending
                nextq = g * NQUAD + q + 2
                weights = [("o", q * QH + 3)]
                if nextq < NG * NQUAD:
                    weights += [("q", nextq % NQUAD * QH + h) for h in range(3)]
                elif nextq == NG * NQUAD:
                    weights += [("o", (q + 1) * QH + h) for h in range(3)]
                self.project(g, q, weights, beside, feed_forward.go_on if u == UNITS else None)
                if q == NQUAD - 1:
                    self.spill_x1(g)
                pending = None
            if u >= UNITS:
                break
            if quad == 0 and group > 0:
                if i == 0:
                    self.load_ctxT(group * GB + 3)
                elif i == 1:
                    self.load_ctxN(group * GB + 3)
            if i == 1 and qn < NG * NQUAD:
                self.fetch_wk(qn % NQUAD)
            if i == GB - 1:
                pending = (group, quad)
        self.steps = [f for j in range(GB) for f in self.ln2(NG - 1, j)]


class FeedForward:

    def __init__(self, b, s, attention):
        self.b, self.attention = b, attention
        sb = lambda name, shape, dt=F32: b.sb(s, name, shape, dt)
        pair = lambda name, shape: (sb(name + "_hi", shape, F32R), sb(name + "_lo", shape, F32R))
        names = ("gate", "up", "down")
        weights, packed, scale = ([[], [], []] for _ in range(3))

        def weight_places(i):
            for k, n in enumerate(names):
                weights[k].append(pair(f"{n}{i}", [P, 4 * 2 * P]))

        def code_places(i):
            for k, n in enumerate(names):
                packed[k].append(sb(f"{n}_packed{i}", [P, 4 * P], I32))
                scale[k].append(sb(f"{n}_scale{i}", [P, 4 * P]))

        code_places(0)
        t16 = lambda name, dt: Place(sb(name, [P, 4 * P], dt))
        self.sign, self.mag = t16("sign", I16), t16("mag", I16)
        self.half, self.over4, self.over6 = t16("half", BF16), t16("over4", BF16), t16("over6", BF16)
        self.value = Turns([sb(f"value{i}", [P, 4 * P], BF16) for i in range(2)])
        self.wide = Turns([sb(f"wide{i}", [P, 4 * P]) for i in range(2)])
        weight_places(0)
        self.xT = pair("xT", [P, DC, TOKENS])
        self.x_raw = Place(sb("xT_raw", [P, DC, CT]))
        self.x_ready = [None] * NCHUNK
        self.sq = Turns([sb(f"sq{i}", [P, CT]) for i in range(2)])
        self.tanh = Turns([sb(f"tanh{i}", [P, CT]) for i in range(2)])
        self.act = Turns([sb(f"act{i}", [P, CT]) for i in range(2)])
        self.inter = Turns([pair(f"inter{i}", [P, CT]) for i in range(4)])
        self.yT = sb("yT", [P, DC, TOKENS])
        self.y_done = [[] for _ in range(NCHUNK)]
        weight_places(1)
        code_places(1)
        self.weights, self.packed, self.scale = ([Turns(t) for t in x] for x in (weights, packed, scale))

    def fetch_x(self, ch):
        b = self.b
        b.sp.wait(*self.x_raw.last_use, *self.attention.x2_spilled[ch])
        self.x_fetched = b.load(self.x_raw.t[:, :, :], b.d["x2T"][:, :, ch * CT:(ch + 1) * CT], "d_x2T")

    def split_x(self, ch):
        b, cols = self.b, slice(ch * CT, (ch + 1) * CT)
        self.x_raw.last_use = self.x_ready[ch] = b.split(
            self.xT[0][:, :, cols], self.xT[1][:, :, cols], self.x_raw.t[:, :, :], b.act, b.dve, "s_xT", [self.x_fetched])

    def load_y(self, ch):
        b, cols = self.b, slice(ch * CT, (ch + 1) * CT)
        b.sp.wait(*self.attention.x1_spilled[ch])
        self.y_done[ch] = [b.load(self.yT[:, :, cols], b.d["x1T"][:, :, cols], f"d_yT{ch}")]

    def fetch(self, jt):
        b, self.fetched = self.b, []
        for k, name in enumerate(("gate", "up", "down")):
            packed, scale = self.packed[k].next(), self.scale[k].next()
            b.sp.wait(*packed.last_use, *scale.last_use)
            m = [b.load(packed.t[:, :], b.d[name + "_packed"][:, jt, :], f"d_{name}{jt % 2}"),
                 b.load(scale.t[:, :], b.d[name + "_scales"][:, jt, :].unsqueeze(1).broadcast_to([8, 16, 4 * P]),
                        f"d_{name}_s{jt % 2}")]
            self.fetched.append((packed, scale, m))

    def decode(self, k, nibble):
        b, kept = self.b, {}
        count = b.count("s_decode")
        dve = lambda emit: b.dve.do(emit, count)
        packed, scale, ready = self.fetched[k]
        codes = packed.t[:, :].bitcast(I16)[:, 0:8 * P:2]
        sign, mag, half, over4, over6 = (x.t[:, :] for x in (self.sign, self.mag, self.half, self.over4, self.over6))

        def bits():
            b.dve.wait(*ready, *self.sign.last_use, *self.mag.last_use)
            dve(lambda e: e.tensor_scalar(sign, codes, 8 << 4 * nibble, 12 - 4 * nibble, ALU.bitwise_and,
                                          ALU.logical_shift_left))
            m = dve(lambda e: e.tensor_scalar(mag, codes, 4 * nibble, 7, ALU.logical_shift_right, ALU.bitwise_and))
            b.act.wait(m, *self.half.last_use)
            self.mag.last_use = kept["half"] = [b.act.do(lambda e: e.activation(half, mag, ACT.Copy, scale=0.5),
                                                         b.count("s_half"))]
            kept["mag"] = m

        def over():
            b.dve.wait(kept["mag"])
            dve(lambda e: e.tensor_scalar(over4, mag, 4.0, 0.5, ALU.max, ALU.mult))
            kept["over"] = dve(lambda e: e.tensor_scalar(over6, mag, 7.0, -2.0, ALU.is_ge, ALU.add))

        def both():
            b.dve.wait(kept["over"])
            kept["both"] = dve(lambda e: e.tensor_tensor(over4, over4, over6, ALU.add))

        def total():
            value = kept["value"] = self.value.next()
            b.dve.wait(kept["both"], *kept["half"], *value.last_use)
            m = dve(lambda e: e.tensor_tensor(value.t[:, :], over4, half, ALU.add))
            self.half.last_use = kept["total"] = [m]

        def signed():
            value = kept["value"]
            v = value.t[:, :].bitcast(I16)
            b.dve.wait(*kept["total"])
            m = dve(lambda e: e.tensor_tensor(v, v, sign, ALU.bitwise_or))
            self.sign.last_use = [m]
            wide = self.wide.next()
            b.pool.wait(m, *ready, *wide.last_use)
            m = b.pool.do(lambda e: e.tensor_tensor(wide.t[:, :], value.t[:, :], scale.t[:, :], ALU.mult),
                          b.count("s_scaled"))
            value.last_use = kept["scaled"] = [m]
            kept["wide"] = wide
            if nibble == 1:
                packed.last_use = scale.last_use = [m]

        def placed():
            wide = kept["wide"]
            if nibble == 0:
                slot = self.weights[k].next()
                b.act.wait(*slot.last_use)
                b.pool.wait(*slot.last_use)
                self.building[k] = (slot, [])
            slot, marks = self.building[k]
            if k < 2:
                view = lambda t: t[:, :].rearrange("p (r z n) -> p r z n", r=2, z=2)[:, :, nibble, :]
                src = wide.t[:, :].rearrange("p (r n) -> p r n", r=2)
            else:
                view = lambda t: t[:, :].rearrange("p (z n) -> p z n", z=2)[:, nibble, :]
                src = wide.t[:, :]
            wide.last_use = b.split(view(slot.t[0]), view(slot.t[1]), src, b.act, b.pool, "s_weight", kept["scaled"])
            marks += wide.last_use

        return [bits, over, both, total, signed, placed]

    def decoding(self):
        steps, placed = [], []
        for k in range(3):
            for nibble in range(2):
                piece = self.decode(k, nibble)
                steps += piece[:2] + placed + piece[2:-1]
                placed = piece[-1:]
        return steps + placed

    def chores(self, n):
        for _ in range(min(n, len(self.waiting))):
            self.waiting.pop(0)()

    def gate_up(self, ch, beside):
        b = self.b
        cols = slice(ch * CT, (ch + 1) * CT)
        xh, xl = (t[:, :, cols] for t in self.xT)
        self.inters = []
        for z in range(2):
            beside(ch, z)
            psums = []
            for k, name in enumerate(("s_gate", "s_up")):
                slot, ready = self.current[k]
                wh, wl = (t[:, :].rearrange("p (c n) -> p c n", c=DC) for t in slot.t)
                bank = b.banks.next()
                b.pe.wait(*bank.last_use)
                b.pe.wait(*ready, *self.x_ready[ch])
                ns = slice(z * P, (z + 1) * P)
                m = b.matmul3(bank.t[:, 0:CT], [(wh[:, c, ns], wl[:, c, ns], xh[:, c, :], xl[:, c, :]) for c in range(DC)],
                              b.count(name))
                slot.last_use = [m]
                psums.append((bank, bank.t[:, 0:CT], m))
            (gbank, g, mg), (ubank, u, mu) = psums
            sq, th, ac = self.sq.next(), self.tanh.next(), self.act.next()
            b.act.wait(*sq.last_use, mg)
            m = b.act.do(lambda e, o=sq.t, g=g: e.activation(o[:, :], g, ACT.Square), b.count("s_g2"))
            b.act.wait(m)
            m = b.act.do(lambda e, o=sq.t: e.activation(o[:, :], o[:, :], ACT.Copy, bias=GELU_C, scale=GELU_A * GELU_C),
                         b.count("s_poly"))
            b.dve.wait(m)
            m = b.dve.do(lambda e, o=sq.t, g=g: e.tensor_tensor(o[:, :], g, o[:, :], ALU.mult), b.count("s_arg"))
            b.act.wait(*th.last_use, m)
            m = b.act.do(lambda e, o=th.t, i=sq.t: e.activation(o[:, :], i[:, :], ACT.Tanh), b.count("s_tanh"))
            sq.last_use = [m]
            self.chores(6)
            b.dve.wait(*ac.last_use, m)
            m = b.dve.do(lambda e, o=ac.t, i=th.t, g=g: e.scalar_tensor_tensor(out=o[:, :], in0=i[:, :], scalar=1.0, in1=g,
                                                                              op0=ALU.add, op1=ALU.mult), b.count("s_gelu"))
            th.last_use = gbank.last_use = [m]
            b.dve.wait(m, mu)
            m = b.dve.do(lambda e, o=ac.t, u=u: e.scalar_tensor_tensor(out=o[:, :], in0=o[:, :], scalar=0.5, in1=u,
                                                                       op0=ALU.mult, op1=ALU.mult), b.count("s_inter"))
            ubank.last_use = [m]
            it = self.inter.next()
            b.act.wait(*it.last_use)
            b.pool.wait(*it.last_use)
            ac.last_use = b.split(it.t[0][:, :], it.t[1][:, :], ac.t[:, :], b.act, b.pool, "s_inters", [m])
            self.inters.append((it, ac.last_use))

    def down(self, ch, down, inters, last):
        b = self.b
        cols = slice(ch * CT, (ch + 1) * CT)
        slot, ready = down
        wh, wl = (t[:, :].rearrange("p (z n) -> p z n", z=2) for t in slot.t)
        b.pe.wait(*ready, *(m for _, r in inters for m in r))
        for c in range(DC):
            bank = b.banks.next()
            b.pe.wait(*bank.last_use)
            cs = slice(c * P, (c + 1) * P)
            m = b.matmul3(bank.t[:, 0:CT], [(wh[:, z, cs], wl[:, z, cs], inters[z][0].t[0][:, :], inters[z][0].t[1][:, :])
                                            for z in range(2)], b.count("s_down"))
            b.dve.wait(m, *self.y_done[ch])
            md = b.dve.do(lambda e, c=c, k=bank: e.tensor_tensor(self.yT[:, c, cols], k.t[:, 0:CT], self.yT[:, c, cols],
                                                                 ALU.add), b.count("s_yT_sum"))
            bank.last_use = [md]
        slot.last_use = [m]
        for it, _ in inters:
            it.last_use = [m]
        self.y_done[ch] = [md]
        if last:
            b.sp.wait(md)
            self.out_marks.append(b.sp.do(lambda e: e.dma_start(b.d["out"][:, :, cols], self.yT[:, :, cols]),
                                          b.count(f"d_out{ch}"), 16))

    def begin_codes(self):
        self.b.sp.wait(*self.b.all_marks())
        self.fetch(0)

    def begin(self):
        b = self.b
        self.out_marks, self.building = [], [None] * 3
        so_far = b.all_marks()
        for q in (b.act, b.dve, b.pool):
            q.wait(*so_far)
        self.waiting = self.decoding()

    def go_on(self):
        b = self.b
        for q in (b.act, b.dve, b.pool, b.sp):
            q.wait(*self.attention.units_done)
        self.fetch_x(0)
        self.split_x(0)

    def beside_first_tile(self, ch, z):
        self.attention.steps_on()
        if z == 1 and ch + 1 < NCHUNK:
            self.split_x(ch + 1)
            if ch + 2 < NCHUNK - 1:
                self.fetch_x(ch + 2)

    def run(self):
        b = self.b
        b.banks.places = b.slow_banks.places + b.banks.places
        projected = [b.count(n).mark() for n in ("s_o", "s_oT_hi", "s_oT_lo", "s_out", "s_wv_hi", "s_wv_lo",
                                                 "s_headw_hi", "s_headw_lo")]
        for q in (b.act, b.dve, b.pool, b.sp):
            q.wait(*projected)
        self.fetch_x(1)
        self.chores(len(self.waiting))
        for ch in range(NCHUNK - 1):
            self.load_y(ch)
        prev = None
        for jt in range(JT):
            self.current = list(self.building)
            for ch in range(NCHUNK):
                if ch == 0 and jt + 1 < JT:
                    self.fetch(jt + 1)
                if ch == 1 and jt + 1 < JT:
                    self.waiting = self.decoding()
                self.gate_up(ch, self.beside_first_tile if jt == 0 else lambda ch, z: None)
                step = (ch, self.current[2], self.inters, jt == JT - 1)
                if jt == 0 and ch + 2 == NCHUNK - 1:
                    self.attention.steps_on()
                    self.fetch_x(ch + 2)
                    self.load_y(ch + 2)
                if prev:
                    self.down(*prev)
                prev = step
            self.chores(len(self.waiting))
        self.down(*prev)
        b.sp.wait(*self.out_marks)


def build(nc, d):
    with ExitStack() as ctx:
        b = Builder(nc, ctx, d)
        build_constants(b, ctx)
        with ExitStack() as s:
            attention = Attention(b, s, ctx)
        with ExitStack() as s:
            ffn = FeedForward(b, s, attention)
            attention.run(ffn)
            ffn.run()
            with nc.Block() as block:
                block.sync(b.sp.replay)
                block.tensor(b.pe.replay)
                block.scalar(b.act.replay)
                block.vector(b.dve.replay)
                block.gpsimd(b.pool.replay)


def kernel(**inputs):
    import concourse.bacc as bacc
    from concourse.bass_utils import run_bass_kernel_spmd

    a = {k: np.asarray(v) for k, v in inputs.items()}
    x, ctxs = a["x"], a["ctx_1024"]
    flat = x.reshape(TOKENS, DIM)

    def rows_by_byte(w):
        return w.reshape(JT, P, 2, 2, P).transpose(4, 0, 3, 2, 1).reshape(P, JT, 4 * P)

    def scales_by_block(w):
        return w.reshape(JT, P, 2, 2, 8).transpose(4, 0, 3, 2, 1).reshape(8, JT, 4 * P)

    arrays = {
        "x": x, "xT": flat.reshape(TOKENS, DC, P).transpose(2, 1, 0),
        "ctx": ctxs, "ctxT": ctxs.reshape(BATCH, SKV, CC, P).transpose(0, 3, 2, 1),
        "Wq": a["L0_xattn_Wq"], "Wk": a["L0_xattn_Wk"], "Wv": a["L0_xattn_Wv"], "Wo": a["L0_xattn_Wo"],
        "gq": a["L0_xattn_gq"].reshape(HD, 1), "gk": a["L0_xattn_gk"].reshape(HD, 1),
        "gate_packed": rows_by_byte(a["L0_ffn_gate_W_packed"]), "gate_scales": scales_by_block(a["L0_ffn_gate_scales"]),
        "up_packed": rows_by_byte(a["L0_ffn_up_W_packed"]), "up_scales": scales_by_block(a["L0_ffn_up_scales"]),
        "down_packed": a["L0_ffn_down_W_packed"].reshape(DIM, JT, P).transpose(2, 1, 0),
        "down_scales": a["L0_ffn_down_scales"].reshape(DIM, JT, 8).transpose(2, 1, 0),
    }
    arrays = {k: np.ascontiguousarray(v) for k, v in arrays.items()}
    nc = bacc.Bacc("TRN2", target_bir_lowering=False, num_devices=1)
    d = {k: nc.dram_tensor(f"in_{k}", v.shape, mybir.dt.from_np(v.dtype), kind="ExternalInput").ap()
         for k, v in arrays.items()}
    d["out"] = nc.dram_tensor("out_yT", (P, DC, TOKENS), F32, kind="ExternalOutput").ap()
    d["x1T"] = nc.dram_tensor("spill_x1T", (P, DC, TOKENS), F32, kind="Internal").ap()
    d["x2T"] = nc.dram_tensor("spill_x2T", (P, DC, TOKENS), F32, kind="Internal").ap()
    build(nc, d)
    r = run_bass_kernel_spmd(nc, [{f"in_{k}": v for k, v in arrays.items()}], core_ids=[0])
    out = r.results[0]["out_yT"]
    return out.transpose(2, 1, 0).reshape(BATCH, SQ, DIM)
```
